# Optimizing a Trainium2 kernel written in Bass

```python
import numpy as np
import jax
import jax.numpy as jnp

def _softmax(x, axis=-1):
    return jax.nn.softmax(x, axis=axis)

def _gelu(x):
    return jax.nn.gelu(x, approximate=True)

def _silu(x):
    return jax.nn.silu(x)

def _sigmoid(x):
    return jax.nn.sigmoid(x)

def _layernorm(x, axis=-1, eps=1e-05):
    m = jnp.mean(x, axis=axis, keepdims=True)
    v = jnp.var(x, axis=axis, keepdims=True)
    return (x - m) / jnp.sqrt(v + eps)

def _scatter_add(tgt, idx, src, axis=0):
    return tgt.at[idx].add(src)

def _segment_sum(src, seg, n):
    return jax.ops.segment_sum(src, seg, n)
kernel_name = 'mk_pixart_seq_d2_seqx_r8_9e6ca7'

def setup_inputs(seed: int=0):
    np.random.seed(seed)
    _w = jnp.asarray

    def _rec_inputs():
        import jax
        import jax.numpy as jnp
        _rk = jax.random.key(seed)
        x = -0.0003929 + 0.9999 * jax.random.normal(jax.random.fold_in(_rk, 1), (4, 256, 128), jnp.float32)
        _lenS = 256 - jax.random.randint(jax.random.fold_in(_rk, 7), (4,), 0, max(1, 256 // 4) + 1, jnp.int32)
        _lenS2 = 512 - jax.random.randint(jax.random.fold_in(_rk, 8), (4,), 0, max(1, 512 // 4) + 1, jnp.int32)
        cond_1024 = 0.00782532 + 1.00527 * jax.random.normal(jax.random.fold_in(_rk, 11), (4, 128), jnp.float32)
        _ctx_1024P = jax.random.normal(jax.random.fold_in(_rk, 12), (4, 16, 128), jnp.float32)
        _ctx_1024c = jax.random.dirichlet(jax.random.fold_in(_rk, 512), 0.3 * jnp.ones((16,), jnp.float32), (4, 512))
        _ctx_1024t = jnp.einsum('bsk,bkd->bsd', _ctx_1024c, _ctx_1024P)
        _ctx_1024t = _ctx_1024t * jax.lax.rsqrt(jnp.mean(jnp.square(_ctx_1024t)) + 1e-12) * 0.953939
        ctx_1024 = -0.000761806 + 0.999296 * (_ctx_1024t + 0.3 * jax.random.normal(jax.random.fold_in(_rk, 612), (4, 512, 128), jnp.float32))
        return (x, cond_1024, ctx_1024)
    x, cond_1024, ctx_1024 = _rec_inputs()

    def _L0_xcond_setup():
        import jax, jax.numpy as jnp
        import numpy as np
        H = 128
        RH = 2 * H
        E = 3
        B, T, P = (8, 256, 64)
        LN_EPS = 1e-05

        def _layer_norm(x, gamma, beta):
            mu = jnp.mean(x, axis=-1, keepdims=True)
            var = jnp.mean(jnp.square(x - mu), axis=-1, keepdims=True)
            return (x - mu) * jax.lax.rsqrt(var + LN_EPS) * gamma + beta
        key = jax.random.key(seed)
        ks = jax.random.split(key, 24)
        s = lambda fan_in: 1.0 / np.sqrt(fan_in)
        inp = {'mix_hidden_states': jax.random.normal(ks[0], (B, T, H), jnp.float32), 'global_anchor': jax.random.normal(ks[1], (B, H), jnp.float32), 'prototype_bank': jax.random.normal(ks[2], (B, P, H), jnp.float32), 'ln_gamma': jnp.ones((H,), jnp.float32), 'ln_beta': jnp.zeros((H,), jnp.float32), 'Wq': jax.random.normal(ks[3], (H, H), jnp.float32) * s(H), 'Wk': jax.random.normal(ks[4], (H, H), jnp.float32) * s(H), 'Wv': jax.random.normal(ks[5], (H, H), jnp.float32) * s(H), 'router_W': jax.random.normal(ks[6], (3 * H, E), jnp.float32) * s(3 * H), 'router_b': jnp.zeros((E,), jnp.float32), 'e_w1': jax.random.normal(ks[7], (E, 3 * H, RH), jnp.float32) * s(3 * H), 'e_b1': jnp.zeros((E, RH), jnp.float32), 'e_w2': jax.random.normal(ks[8], (E, RH, H), jnp.float32) * s(RH), 'e_b2': jnp.zeros((E, H), jnp.float32), 'gate_w1': jax.random.normal(ks[9], (3 * H, H), jnp.float32) * s(3 * H), 'gate_b1': jnp.zeros((H,), jnp.float32), 'gate_w2': jax.random.normal(ks[10], (H, H), jnp.float32) * s(H), 'gate_b2': jnp.zeros((H,), jnp.float32), 'out_w': jax.random.normal(ks[11], (H, H), jnp.float32) * s(H), 'out_b': jnp.zeros((H,), jnp.float32)}
        return inp
    _L0_xcond_all = _L0_xcond_setup()
    _L0_xcond_in = {k: v for k, v in _L0_xcond_all.items() if k in ('ln_gamma', 'ln_beta', 'Wq', 'Wk', 'Wv', 'router_W', 'router_b', 'e_w1', 'e_b1', 'e_w2', 'e_b2', 'gate_w1', 'gate_b1', 'gate_w2', 'gate_b2', 'out_w', 'out_b')}
    del _L0_xcond_all

    def _L1_xcond_setup():
        import jax, jax.numpy as jnp
        import numpy as np
        EPS = 1e-05

        def _ada_ln(x, c, W_ss, b_ss):
            mu = jnp.mean(x, axis=-1, keepdims=True)
            var = jnp.mean((x - mu) ** 2, axis=-1, keepdims=True)
            h = (x - mu) / jnp.sqrt(var + EPS)
            ss = jax.nn.silu(c) @ W_ss + b_ss
            scale, bias = jnp.split(ss, 2, axis=-1)
            return (1.0 + scale)[:, None, :] * h + bias[:, None, :]
        key = jax.random.key(seed)
        ks = jax.random.split(key, 12)
        B, Lq, Lkv, H = (8, 256, 64, 128)
        s = 0.02
        return {'x_q': jax.random.normal(ks[0], (B, Lq, H), jnp.float32), 'x_kv': jax.random.normal(ks[1], (B, Lkv, H), jnp.float32), 't_vec': jax.random.normal(ks[2], (B, H), jnp.float32), 'Wq': jax.random.normal(ks[3], (H, H), jnp.float32) * s, 'bq': jnp.zeros((H,), jnp.float32), 'Wkv': jax.random.normal(ks[4], (H, 2 * H), jnp.float32) * s, 'bkv': jnp.zeros((2 * H,), jnp.float32), 'Wp': jax.random.normal(ks[5], (H, H), jnp.float32) * s, 'bp': jnp.zeros((H,), jnp.float32), 'Wss_q': jax.random.normal(ks[6], (H, 2 * H), jnp.float32) * s, 'bss_q': jnp.zeros((2 * H,), jnp.float32), 'Wss_kv': jax.random.normal(ks[7], (H, 2 * H), jnp.float32) * s, 'bss_kv': jnp.zeros((2 * H,), jnp.float32)}
    _L1_xcond_all = _L1_xcond_setup()
    _L1_xcond_in = {k: v for k, v in _L1_xcond_all.items() if k in ('Wq', 'bq', 'Wkv', 'bkv', 'Wp', 'bp', 'Wss_q', 'bss_q', 'Wss_kv', 'bss_kv')}
    del _L1_xcond_all
    return {'x': x, 'cond_1024': cond_1024, 'ctx_1024': ctx_1024, 'L0_xcond_ln_gamma': _L0_xcond_in['ln_gamma'], 'L0_xcond_ln_beta': _L0_xcond_in['ln_beta'], 'L0_xcond_Wq': _L0_xcond_in['Wq'], 'L0_xcond_Wk': _L0_xcond_in['Wk'], 'L0_xcond_Wv': _L0_xcond_in['Wv'], 'L0_xcond_router_W': _L0_xcond_in['router_W'], 'L0_xcond_router_b': _L0_xcond_in['router_b'], 'L0_xcond_e_w1': _L0_xcond_in['e_w1'], 'L0_xcond_e_b1': _L0_xcond_in['e_b1'], 'L0_xcond_e_w2': _L0_xcond_in['e_w2'], 'L0_xcond_e_b2': _L0_xcond_in['e_b2'], 'L0_xcond_gate_w1': _L0_xcond_in['gate_w1'], 'L0_xcond_gate_b1': _L0_xcond_in['gate_b1'], 'L0_xcond_gate_w2': _L0_xcond_in['gate_w2'], 'L0_xcond_gate_b2': _L0_xcond_in['gate_b2'], 'L0_xcond_out_w': _L0_xcond_in['out_w'], 'L0_xcond_out_b': _L0_xcond_in['out_b'], 'L1_xcond_Wq': _L1_xcond_in['Wq'], 'L1_xcond_bq': _L1_xcond_in['bq'], 'L1_xcond_Wkv': _L1_xcond_in['Wkv'], 'L1_xcond_bkv': _L1_xcond_in['bkv'], 'L1_xcond_Wp': _L1_xcond_in['Wp'], 'L1_xcond_bp': _L1_xcond_in['bp'], 'L1_xcond_Wss_q': _L1_xcond_in['Wss_q'], 'L1_xcond_bss_q': _L1_xcond_in['bss_q'], 'L1_xcond_Wss_kv': _L1_xcond_in['Wss_kv'], 'L1_xcond_bss_kv': _L1_xcond_in['bss_kv']}

def reference(x, cond_1024, ctx_1024, L0_xcond_ln_gamma, L0_xcond_ln_beta, L0_xcond_Wq, L0_xcond_Wk, L0_xcond_Wv, L0_xcond_router_W, L0_xcond_router_b, L0_xcond_e_w1, L0_xcond_e_b1, L0_xcond_e_w2, L0_xcond_e_b2, L0_xcond_gate_w1, L0_xcond_gate_b1, L0_xcond_gate_w2, L0_xcond_gate_b2, L0_xcond_out_w, L0_xcond_out_b, L1_xcond_Wq, L1_xcond_bq, L1_xcond_Wkv, L1_xcond_bkv, L1_xcond_Wp, L1_xcond_bp, L1_xcond_Wss_q, L1_xcond_bss_q, L1_xcond_Wss_kv, L1_xcond_bss_kv):
    import jax
    import jax.numpy as jnp

    def _L0_xcond_ref(mix_hidden_states, global_anchor, prototype_bank, ln_gamma, ln_beta, Wq, Wk, Wv, router_W, router_b, e_w1, e_b1, e_w2, e_b2, gate_w1, gate_b1, gate_w2, gate_b2, out_w, out_b):
        import jax, jax.numpy as jnp
        import numpy as np
        H = 128
        RH = 2 * H
        E = 3
        B, T, P = (8, 256, 64)
        LN_EPS = 1e-05

        def _layer_norm(x, gamma, beta):
            mu = jnp.mean(x, axis=-1, keepdims=True)
            var = jnp.mean(jnp.square(x - mu), axis=-1, keepdims=True)
            return (x - mu) * jax.lax.rsqrt(var + LN_EPS) * gamma + beta
        x = mix_hidden_states
        nx = _layer_norm(x, ln_gamma, ln_beta)
        q = nx @ Wq
        k = prototype_bank @ Wk
        v = prototype_bank @ Wv
        scores = jnp.einsum('bth,bph->btp', q, k) * H ** (-0.5)
        weights = jax.nn.softmax(scores, axis=-1)
        evidence = jnp.einsum('btp,bph->bth', weights, v)
        anchor = jnp.broadcast_to(global_anchor[:, None, :], nx.shape)
        combined = jnp.concatenate([nx, evidence, anchor], axis=-1)
        router_logits = combined @ router_W + router_b
        router_probs = jax.nn.softmax(router_logits, axis=-1)
        h = jax.nn.silu(jnp.einsum('btc,ecr->bter', combined, e_w1) + e_b1)
        expert_out = jnp.einsum('bter,erh->bteh', h, e_w2) + e_b2
        routed = jnp.sum(expert_out * router_probs[..., None], axis=-2)
        g = jax.nn.sigmoid(jax.nn.silu(combined @ gate_w1 + gate_b1) @ gate_w2 + gate_b2)
        refined_delta = g * (routed @ out_w + out_b)
        return x + refined_delta

    def _L1_xcond_ref(x_q, x_kv, t_vec, Wq, bq, Wkv, bkv, Wp, bp, Wss_q, bss_q, Wss_kv, bss_kv):
        import jax, jax.numpy as jnp
        import numpy as np
        EPS = 1e-05

        def _ada_ln(x, c, W_ss, b_ss):
            mu = jnp.mean(x, axis=-1, keepdims=True)
            var = jnp.mean((x - mu) ** 2, axis=-1, keepdims=True)
            h = (x - mu) / jnp.sqrt(var + EPS)
            ss = jax.nn.silu(c) @ W_ss + b_ss
            scale, bias = jnp.split(ss, 2, axis=-1)
            return (1.0 + scale)[:, None, :] * h + bias[:, None, :]
        B, Lq, H = x_q.shape
        Lkv = x_kv.shape[1]
        nh = 16
        dh = H // nh
        xq = _ada_ln(x_q, t_vec, Wss_q, bss_q)
        xkv = _ada_ln(x_kv, t_vec, Wss_kv, bss_kv)
        q = (xq @ Wq + bq).reshape(B, Lq, nh, dh)
        kv = (xkv @ Wkv + bkv).reshape(B, Lkv, 2, nh, dh)
        k = kv[:, :, 0]
        v = kv[:, :, 1]
        scores = jnp.einsum('bqhd,bkhd->bhqk', q, k) / jnp.sqrt(jnp.float32(dh))
        attn = jax.nn.softmax(scores, axis=-1)
        out = jnp.einsum('bhqk,bkhd->bqhd', attn, v).reshape(B, Lq, H)
        return x_q + (out @ Wp + bp)
    x = _L0_xcond_ref(x, cond_1024, ctx_1024, L0_xcond_ln_gamma, L0_xcond_ln_beta, L0_xcond_Wq, L0_xcond_Wk, L0_xcond_Wv, L0_xcond_router_W, L0_xcond_router_b, L0_xcond_e_w1, L0_xcond_e_b1, L0_xcond_e_w2, L0_xcond_e_b2, L0_xcond_gate_w1, L0_xcond_gate_b1, L0_xcond_gate_w2, L0_xcond_gate_b2, L0_xcond_out_w, L0_xcond_out_b)
    x = _L1_xcond_ref(x, ctx_1024, cond_1024, L1_xcond_Wq, L1_xcond_bq, L1_xcond_Wkv, L1_xcond_bkv, L1_xcond_Wp, L1_xcond_bp, L1_xcond_Wss_q, L1_xcond_bss_q, L1_xcond_Wss_kv, L1_xcond_bss_kv)
    return x

_drawn_inputs = setup_inputs


def setup_inputs(seed=0):
    import zlib

    import numpy as np

    out = dict(_drawn_inputs(seed))
    spreads = {'L0_xcond_ln_gamma': (1.0, 0.2),
     'L0_xcond_ln_beta': (0.0, 0.617),
     'L0_xcond_router_b': (0.0, 0.8),
     'L0_xcond_e_b1': (0.0, 0.362),
     'L0_xcond_e_b2': (0.0, 0.1),
     'L0_xcond_gate_b1': (0.0, 0.8),
     'L0_xcond_gate_b2': (0.0, 0.8),
     'L0_xcond_out_b': (0.0, 0.1),
     'L1_xcond_bq': (0.0, 2.0),
     'L1_xcond_bkv': (0.0, 0.34),
     'L1_xcond_bp': (0.0, 0.1),
     'L1_xcond_bss_q': (0.0, 2.0),
     'L1_xcond_bss_kv': (0.0, 0.8)}
    factors = {'L1_xcond_Wq': 8.0, 'L1_xcond_Wss_q': 24.132, 'L1_xcond_Wss_kv': 7.301}
    for name, (base, spread) in spreads.items():
        noise = np.random.default_rng([zlib.crc32(name.encode()), seed]).standard_normal(out[name].shape)
        drawn = base * np.exp(spread * noise) if base else spread * noise
        out[name] = jnp.asarray(drawn.astype(out[name].dtype))
    for name, factor in factors.items():
        out[name] = (out[name] * factor).astype(out[name].dtype)
    return out
```

```python
from contextlib import ExitStack

import concourse.bass as bass
from concourse import mybir

F32 = mybir.dt.float32
BF16 = mybir.dt.bfloat16
ACT = mybir.ActivationFunctionType
ALU = mybir.AluOpType
AX_X = mybir.AxisListType.X

P = 128
B = 4
T, TC = 256, 2
S, SC = 512, 4
E, RC = 3, 2
NH, DH = 16, 8
GH = 4
NG = NH // GH
PV_COLS, PV_SILU, PV_SPREAD, PV_W2T, PV_ALL = 1, 3, 4, 5, 9
QT = 32
NZ = E * RC + 1
NP = 3
KR = NP * NP * DH
EPS = 1e-5
SCALE0 = float(P) ** -0.5
SCALE1 = float(DH) ** -0.5

R_B1, R_GB1, R_GAMMA, R_BETA, R_BQ, R_BK, R_BV, R_SSQ, R_SSK, R_COND, R_EB2 = 0, 6, 7, 8, 9, 10, 11, 12, 14, 16, 20
NR = 23
V_Z, V_HALF, V_ADA, NV = 0, NZ, 2 * NZ, 2 * NZ + 4

SPARE = ["ctxT", "nxT", "qm", "s0_0", "s0_1", "hkvT", "kproj", "p0T_0", "p0T_1", "vproj", "pc",
         "hid_0", "hid_1", "hid_2", "hid_3", "lgT", "eo_0", "eo_1", "xqT", "qproj"]
HALF = len(SPARE) // 2


def spare_bank(name):
    return SPARE.index(name) % 2


CREDIT = 16


class Chain:

    def __init__(self, eng, sem, per):
        self.eng, self.sem, self.per = eng, sem, per

    def begin(self, b):
        self.base, self.n = b * self.per, 0

    def step(self, ins):
        self.n += 1
        ins.then_inc(self.sem, 1)

    def link(self, ins):
        self.step(ins)
        self.wait()

    def wait(self):
        self.eng.wait_ge(self.sem, self.base + self.n)

    def end(self):
        assert self.n == self.per, (self.n, self.per)


def build(nc, a, out):
    with ExitStack() as ctx:
        def sb(name, shape, dt=F32):
            return ctx.enter_context(nc.sbuf_tensor(name, shape, dt))

        def sem(name):
            return ctx.enter_context(nc.semaphore(name))

        rows = sb("rows", [NR, P])
        cols = sb("cols", [P, NR])
        w_qkv = sb("w_qkv", [P, 3, P])
        w_qkvT = sb("w_qkvT", [P, 3, P])
        w1 = sb("w1", [P, 3, E, RC * P])
        gw1 = sb("gw1", [P, 3, P])
        rw = sb("rw", [P, 3, E])
        rb = sb("rb", [E, 1])
        w2 = sb("w2", [P, E * RC, P])
        w2T = sb("w2T", [P, E * RC, P])
        gw2 = sb("gw2", [P, P])
        ow = sb("ow", [P, P])
        wq1 = sb("wq1", [P, P])
        wkv1 = sb("wkv1", [P, 2 * P])
        wp1 = sb("wp1", [P, P])
        wssq = sb("wssq", [P, 2 * P])
        wssk = sb("wssk", [P, 2 * P])
        m_qk = sb("m_qk", [P, P])
        w1ev = sb("w1ev", [P, E * RC * P])
        gw1ev = sb("gw1ev", [P, P])
        rwev = sb("rwev", [P, E])
        w2o = sb("w2o", [P, E * RC, P])
        bias2 = sb("bias2", [P, E, P])
        bias_g = sb("bias_g", [P, P])
        bias_o = sb("bias_o", [P, P])
        vec_row = sb("vec_row", [1, 2, P])
        ones = sb("ones", [P, P])
        spread = sb("spread", [P, E + 1, P])
        silu_t = sb("silu_t", [P, B])
        silu_c = sb("silu_c", [P, B])
        ident = sb("ident", [P, P])
        identb = sb("identb", [P, P], BF16)
        onesb = sb("onesb", [NP * NH * S // T, T], BF16)
        allv = sb("allv", [P, B, NV])
        rball = sb("rball", [E, B])
        cur = sb("cur", [P, NV])
        rcur = sb("rcur", [E, 1])
        mhalf = sb("mhalf", [P, TC + SC])

        x_sb = sb("x_sb", [P, TC, P])
        c_sb = sb("c_sb", [P, SC, P])
        stats = sb("stats", [P, TC + SC, 6])
        mv = sb("mv", [P, TC + SC, 2])
        ve = sb("ve", [P, TC + SC])
        rstd = sb("rstd", [P, TC + SC])
        xn = sb("xn", [P, TC, P])
        cn = sb("cn", [P, SC, P])
        ctxT = sb("ctxT", [P, S])
        nxT = sb("nxT", [P, T])
        qmT = sb("qmT", [P, T])
        nm0 = sb("nm0", [P, TC])
        sum0 = sb("sum0", [P, TC])
        rs0 = sb("rs0", [P, TC])
        p0 = sb("p0", [P, TC, S])
        p0T = sb("p0T", [P, SC, T])
        pcT = sb("pcT", [P, T])
        tz = sb("tz", [P, 8, T])
        hT = sb("hT", [P, 8, T])
        lg = sb("lg", [E, T])
        rmx = sb("rmx", [P, TC])
        rd = sb("rd", [P, TC, E])
        re = sb("re", [P, TC, E])
        rsum = sb("rsum", [P, TC])
        rinv = sb("rinv", [P, TC])
        pr = sb("pr", [P, TC, E])
        pbt = sb("pbt", [P, TC, E, P])
        pbs = sb("pbs", [P, TC, P])
        pb = sb("pb", [P, TC, P])
        yacc = sb("yacc", [P, 3, TC, P])
        zg = sb("zg", [P, TC, P])
        tg = sb("tg", [P, TC, P])
        ug = sb("ug", [P, TC, P])
        x1 = sb("x1", [P, TC, P])
        st1 = sb("st1", [P, TC, 6])
        mv1 = sb("mv1", [P, TC, 2])
        ve1 = sb("ve1", [P, TC])
        rstd1 = sb("rstd1", [P, TC])
        xn1 = sb("xn1", [P, TC, P])
        resid = sb("resid", [P, TC, P])
        xkvT = sb("xkvT", [P, S])
        xqT = sb("xqT", [P, T])
        kf = sb("kf", [P, S])
        kr = sb("kr", [P, 2, S])
        kp = sb("kp", [P, NP, S], BF16)
        qf = sb("qf", [P, T])
        qr = sb("qr", [P, 2, T])
        qp = sb("qp", [P, NP, T], BF16)
        vst = sb("vst", [P, SC, P])
        vtile = sb("vtile", [P, SC, NH, QT])
        q_st = sb("q_st", [P, NH, T], BF16)
        k_st = sb("k_st", [P, NH, S], BF16)
        probs = sb("probs", [P, 2, GH, SC * T])
        o_sb = sb("o_sb", [P, NG, T])
        rs1 = sb("rs1", [P, TC, NH])
        on = sb("on", [P, TC, P])
        onT = sb("onT", [P, T])
        y_sb = sb("y_sb", [P, TC, P])
        mx = sb("mx", [P, TC, NH])
        mr = sb("mr", [P, 3, TC, NH])
        mparts = sb("mparts", [P, TC, NP, NH], BF16)
        mT = sb("mT", [NP * NH, T], BF16)

        ps = ctx.enter_context(nc.psum_tensor("ps", [P, 8, 512], F32))
        OB, MB = 4, 6

        q_scr = nc.dram_tensor("q_scr", (NP, DH, NH, T), BF16, kind="Internal").ap()
        k_scr = nc.dram_tensor("k_scr", (DH, NP, NH, S), BF16, kind="Internal").ap()

        s_rows = sem("s_rows")
        s_wqkv = sem("s_wqkv")
        s_wall = sem("s_wall")
        s_ident = sem("s_ident")
        s_const = sem("s_const")
        s_zero = sem("s_zero")
        s_ones = sem("s_ones")
        s_pp = sem("s_pp")
        s_pv = sem("s_pv")
        s_ps = sem("s_ps")
        s_x = sem("s_x")
        s_c = sem("s_c")
        s_var = sem("s_var")
        s_rstd = sem("s_rstd")
        s_xn = sem("s_xn")
        s_cn = sem("s_cn")
        s_full = [sem("s_full0"), sem("s_full1")]
        s_done = [sem("s_done0"), sem("s_done1")]
        s_nm0 = sem("s_nm0")
        s_p0 = sem("s_p0")
        s_tz = sem("s_tz")
        s_sg = sem("s_sg")
        s_rd = sem("s_rd")
        s_re = sem("s_re")
        s_pr = sem("s_pr")
        s_pb = sem("s_pb")
        s_zg = sem("s_zg")
        s_tg = sem("s_tg")
        s_x1 = sem("s_x1")
        s_xn1 = sem("s_xn1")
        s_res = sem("s_res")
        s_kp = sem("s_kp")
        s_qp = sem("s_qp")
        s_kscr = sem("s_kscr")
        s_qscr = sem("s_qscr")
        s_st = [sem("s_stA"), sem("s_stB")]
        s_vt = sem("s_vt")
        s_sc = sem("s_sc")
        s_pe = sem("s_pe")
        s_o = sem("s_o")
        s_od = [sem("s_od0"), sem("s_od1")]
        s_post = sem("s_post")
        s_y = sem("s_y")
        s_out = sem("s_out")
        s_gm = sem("s_gm")
        s_gr = sem("s_gr")
        s_mp = sem("s_mp")
        s_mrow = sem("s_mrow")
        s_cv = sem("s_cv")
        s_cm = sem("s_cm")
        s_cx = sem("s_cx")
        s_cc = sem("s_cc")
        s_cg = sem("s_cg")
        s_tick = sem("s_tick")

        free_again = [*s_done, s_o, *s_od, s_pe, s_y, s_x1, s_kscr, s_qscr, *s_st, s_sc, s_gr, s_res, s_vt, s_out]
        ST_DMAS = 2 * NP
        GM = NH * TC

        def need(eng, s, value, hold=False):
            if s in free_again:
                value = value + CREDIT
            eng.wait_ge(s, value)
            if hold:
                eng.sem_inc(s_tick, 1)

        def full(eng, b, name):
            k = SPARE.index(name)
            need(eng, s_full[k % 2], b * HALF + k // 2 + 1)

        def done(eng, b, name, hold=False):
            k = SPARE.index(name)
            need(eng, s_done[k % 2], b * HALF + k // 2 + 1, hold)

        def room(eng, b, name):
            k = SPARE.index(name)
            need(eng, s_done[k % 2], b * HALF + k // 2)

        def bank(name):
            return ps[:, MB + spare_bank(name), :]

        def filled(name, ins):
            ins.then_inc(s_full[spare_bank(name)], 1)

        def emptied(name, ins):
            ins.then_inc(s_done[spare_bank(name)], 1)

        block = ctx.enter_context(nc.Block())

        @block.sync
        def _(sp):
            def v(name, r):
                return a[name].rearrange("(r d) -> r d", r=r)

            def at(t, b):
                return t[b:b + 1] if isinstance(b, int) else t[bass.ds(b, 1)]

            def waits(*pairs):
                for s, x in pairs:
                    need(sp, s, x, hold=not isinstance(x, int))

            def load_batch(b):
                if not (isinstance(b, int) and b == 0):
                    waits((s_x1, b))
                sp.dma_start(x_sb[:], at(a["x"].rearrange("b (c p) d -> b p c d", p=P), b)).then_inc(s_x, 16)
                sp.dma_start(c_sb[:], at(a["ctx_1024"].rearrange("b (c p) d -> b p c d", p=P), b)).then_inc(s_c, 16)

            def stacks(b):
                waits((s_kp, b + 1), (s_st[0], b * ST_DMAS * 16), (s_st[1], b * ST_DMAS * 16))
                for i in range(NP):
                    sp.dma_start(k_scr[:, i, :, :].rearrange("d h t -> h d t"), kp[:, i, :]).then_inc(s_kscr, 16)
                waits((s_qp, b + 1))
                for i in range(NP):
                    sp.dma_start(q_scr[i].rearrange("d h t -> h d t"), qp[:, i, :]).then_inc(s_qscr, 16)
                for half in range(2):
                    h0, h1 = half * NH // 2, (half + 1) * NH // 2
                    waits((s_kscr, (b + 1) * NP * 16), (s_qscr, (b + 1) * NP * 16), (s_sc, (b - 1) * NH + h1))
                    for i in range(NP):
                        r = slice(i * NP * DH, (i + 1) * NP * DH)
                        sp.dma_start(k_st[r, h0:h1, :], k_scr[:, :, h0:h1, :]).then_inc(s_st[half], 16)
                        sp.dma_start(q_st[r, h0:h1, :],
                                     q_scr[i, :, h0:h1, :].rearrange("d h t -> d (h t)").unsqueeze(1)
                                     .to_broadcast([DH, NP, NH // 2 * T])).then_inc(s_st[half], 16)

            def maxima_rows(b):
                waits((s_gr, (b + 1) * (GM + 1)))
                sp.dma_start(q_st[KR:KR + NP, :, :], mT[:]).then_inc(s_mrow, 16)

            def store(b):
                waits((s_y, b + 1))
                sp.dma_start(at(out.rearrange("b (c p) d -> b p c d", p=P), b), y_sb[:]).then_inc(s_out, 16)

            for i, name in enumerate(("L0_xcond_Wq", "L0_xcond_Wk", "L0_xcond_Wv")):
                sp.dma_start(w_qkv[:, i, :], a[name]).then_inc(s_wqkv, 16)
            load_batch(0)
            sp.dma_start(rows[R_B1:R_B1 + E * RC, :],
                         a["L0_xcond_e_b1"].rearrange("e (k r) -> (e k) r", k=RC)).then_inc(s_rows, 16)
            for r, n, name in ((R_GB1, 1, "L0_xcond_gate_b1"), (R_GAMMA, 1, "L0_xcond_ln_gamma"),
                               (R_BETA, 1, "L0_xcond_ln_beta"), (R_BQ, 1, "L1_xcond_bq"), (R_BK, 2, "L1_xcond_bkv"),
                               (R_SSQ, 2, "L1_xcond_bss_q"), (R_SSK, 2, "L1_xcond_bss_kv")):
                sp.dma_start(rows[r:r + n, :], v(name, n)).then_inc(s_rows, 16)
            sp.dma_start(rows[R_COND:R_COND + B, :], a["cond_1024"]).then_inc(s_rows, 16)
            sp.dma_start(rows[R_EB2:R_EB2 + E, :], a["L0_xcond_e_b2"]).then_inc(s_rows, 16)
            for k in range(3):
                sp.dma_start(w1[:, k, :, :], a["L0_xcond_e_w1"].rearrange("e (k c) r -> k c e r", k=3)[k])\
                    .then_inc(s_wall, 16)
            sp.dma_start(gw1[:], a["L0_xcond_gate_w1"].rearrange("(k c) r -> c k r", k=3)).then_inc(s_wall, 16)
            sp.dma_start(rw[:], a["L0_xcond_router_W"].rearrange("(k c) r -> c k r", k=3)).then_inc(s_wall, 16)
            sp.dma_start(w2[:], a["L0_xcond_e_w2"].rearrange("e (k r) h -> r (e k) h", k=RC)).then_inc(s_wall, 16)
            for t, name in ((gw2, "L0_xcond_gate_w2"), (ow, "L0_xcond_out_w"), (wq1, "L1_xcond_Wq"),
                            (wkv1, "L1_xcond_Wkv"), (wp1, "L1_xcond_Wp"), (wssq, "L1_xcond_Wss_q"),
                            (wssk, "L1_xcond_Wss_kv")):
                sp.dma_start(t[:], a[name]).then_inc(s_wall, 16)
            sp.dma_start(rb[:], v("L0_xcond_router_b", E)).then_inc(s_wall, 16)
            sp.dma_start(vec_row[:, 0, :], v("L0_xcond_out_b", 1)).then_inc(s_wall, 16)
            sp.dma_start(vec_row[:, 1, :], v("L1_xcond_bp", 1)).then_inc(s_wall, 16)
            sp.dma_start(bias_g[:], v("L0_xcond_gate_b2", 1).to_broadcast([P, P])).then_inc(s_wall, 16)
            sp.wait_ge(s_const, 1)
            sp.wait_ge(s_zero, 1)
            sp.dma_start(k_st[KR:KR + NP, :, :], onesb[:]).then_inc(s_ones, 16)
            stacks(0)
            with sp.Fori(0, B - 1) as i:
                maxima_rows(i)
                load_batch(i + 1)
                stacks(i + 1)
                store(i)
            maxima_rows(B - 1)
            store(B - 1)
            need(sp, s_out, 16 * B)

        @block.gpsimd
        def _(pool):
            own = Chain(pool, s_cg, 8)

            def before(b):
                own.begin(b)
                need(pool, s_var, 2 * b + 1)
                nc.gpsimd.tensor_tensor(rstd[:], ve[:], mhalf[:], ALU.pow).then_inc(s_rstd, 1)
                need(pool, s_kscr, b * NP * 16, hold=True)
                done(pool, b, "kproj", hold=True)
                own.link(nc.gpsimd.tensor_copy(kp[:, 0, :], kf[:]))
                own.link(nc.gpsimd.tensor_tensor(kr[:, 0, :], kf[:], kp[:, 0, :], ALU.subtract))
                pool.sem_inc(s_tick, 1)
                own.link(nc.gpsimd.tensor_copy(kp[:, 1, :], kr[:, 0, :]))
                own.link(nc.gpsimd.tensor_tensor(kr[:, 1, :], kr[:, 0, :], kp[:, 1, :], ALU.subtract))
                pool.sem_inc(s_tick, 1)
                nc.gpsimd.tensor_copy(kp[:, 2, :], kr[:, 1, :]).then_inc(s_kp, 1)
                for k in range(4):
                    n = min(2, NZ - 2 * k)
                    need(pool, s_tz, 4 * b + k + 1, hold=True)
                    nc.gpsimd.tensor_scalar(tz[:, 2 * k:2 * k + n, :], tz[:, 2 * k:2 * k + n, :], 0.5, 0.5,
                                            ALU.mult, ALU.add).then_inc(s_sg, 1)
                need(pool, s_pr, b + 1, hold=True)
                for t in range(TC):
                    for e in range(E):
                        last = nc.gpsimd.tensor_scalar(pbt[:, t, e, :], bias2[:, e, :], pr[:, t, e:e + 1], 1.0,
                                                       ALU.mult, ALU.mult)
                own.link(last)
                for t in range(TC):
                    last = nc.gpsimd.tensor_tensor(pbs[:, t, :], pbt[:, t, 0, :], pbt[:, t, 1, :], ALU.add)
                own.link(last)
                for t in range(TC):
                    last = nc.gpsimd.tensor_tensor(pb[:, t, :], pbs[:, t, :], pbt[:, t, 2, :], ALU.add)
                last.then_inc(s_pb, 1)
                need(pool, s_var, 2 * b + 2)
                own.step(nc.gpsimd.tensor_tensor(rstd1[:], ve1[:], mhalf[:, 0:TC], ALU.pow))
                own.wait()
                pool.sem_inc(s_rstd, 1)
                need(pool, s_y, b)
                own.link(nc.gpsimd.tensor_tensor(resid[:, 0, :], x1[:, 0, :], bias_o[:], ALU.add))
                nc.gpsimd.tensor_tensor(resid[:, 1, :], x1[:, 1, :], bias_o[:], ALU.add).then_inc(s_res, 1)
                own.end()

            def heads(b):
                done(pool, b, "vproj", hold=True)
                need(pool, s_o, NG * b, hold=True)
                nc.gpsimd.tensor_copy(vtile[:, :, :, 0:DH], vst[:].rearrange("p c (h d) -> p c h d", h=NH))\
                    .then_inc(s_vt, 1)

            for s in free_again:
                pool.sem_inc(s, CREDIT)
            nc.gpsimd.memset(ident[:], 0.0).then_inc(s_cc, 1)
            pool.wait_ge(s_cc, 1)
            nc.gpsimd.affine_select(out=ident[:], in_=ident[:], compare_op=ALU.not_equal, fill=1.0, base=0,
                                    pattern=[[-1, P]], channel_multiplier=1).then_inc(s_ident, 1)
            nc.gpsimd.memset(ones[:], 1.0)
            nc.gpsimd.memset(onesb[:], 1.0)
            nc.gpsimd.memset(mhalf[:], -0.5)
            nc.gpsimd.memset(vtile[:], 0.0).then_inc(s_cc, 1)
            pool.wait_ge(s_cc, 2)
            pool.wait_ge(s_ident, 1)
            nc.gpsimd.tensor_copy(identb[:], ident[:])
            nc.gpsimd.memset(vtile[:, :, :, DH:DH + 1], 1.0).then_inc(s_const, 1)
            before(0)
            with pool.Fori(0, B - 1) as i:
                heads(i)
                before(i + 1)
            heads(B - 1)

        @block.scalar
        def _(act):
            def before(b):
                full(act, b, "ctxT")
                emptied("ctxT", nc.scalar.copy(ctxT[:], bank("ctxT")))
                for t in range(TC):
                    name = f"s0_{t}"
                    need(act, s_nm0, TC * b + t + 1)
                    emptied(name, nc.scalar.activation(p0[:, t, :], bank(name), ACT.Exp, bias=nm0[:, t:t + 1],
                                                       accum_out=sum0[:, t:t + 1]))
                full(act, b, "p0T_0")
                emptied("p0T_0", nc.scalar.copy(p0T[:, :, 0:P], bank("p0T_0").rearrange("p (c t) -> p c t", c=SC)))
                full(act, b, "vproj")
                need(act, s_vt, b, hold=True)
                emptied("vproj", nc.scalar.copy(vst[:].rearrange("p c d -> p (c d)"), bank("vproj")))
                for k in range(4):
                    name = f"hid_{k}"
                    full(act, b, name)
                    for j in range(min(2, NZ - 2 * k)):
                        z = 2 * k + j
                        last = nc.scalar.activation(tz[:, z, :], bank(name)[:, j * T:(j + 1) * T], ACT.Tanh,
                                                    bias=cur[:, V_HALF + z:V_HALF + z + 1], scale=0.5)
                    last.then_inc(s_tz, 1)
                need(act, s_rd, b + 1)
                nc.scalar.activation(re[:], rd[:], ACT.Exp).then_inc(s_re, 1)
                need(act, s_zg, b + 1)
                nc.scalar.activation(tg[:], zg[:], ACT.Tanh, scale=0.5).then_inc(s_tg, 1)

            def head(b, h):
                g, j = divmod(h, GH)
                if j == 0:
                    need(act, s_o, NG * b + g - 1, hold=True)
                need(act, s_sc, NH * b + h + 1)
                pair = 2 * (h % 2)
                nc.scalar.activation(probs[:, g % 2, j, :], ps[:, pair:pair + 2, :].rearrange("p a n -> p (a n)"),
                                     ACT.Exp).then_inc(s_pe, 1)

            nc.scalar.memzero(k_st[64:P, :, :].rearrange("p h t -> p (h t)").bitcast(F32))
            nc.scalar.memzero(q_st[64:P, :, :].rearrange("p h t -> p (h t)").bitcast(F32)).then_inc(s_zero, 1)
            act.wait_ge(s_pv, PV_COLS)
            nc.scalar.activation(silu_t[:], cols[:, R_COND:R_COND + B], ACT.Tanh, scale=0.5).then_inc(s_ps, 1)
            before(0)
            with act.Fori(0, B - 1) as i:
                for h in range(NH):
                    head(i, h)
                before(i + 1)
            for h in range(NH):
                head(B - 1, h)

        @block.tensor
        def _(pe):
            def mm(out, lhsT, rhs, start=True, stop=True):
                return nc.tensor.matmul(out, lhsT, rhs, start=start, stop=stop)

            def turn(out, in_, idn):
                return nc.tensor.transpose(out, in_, idn)

            def prepare():
                step = lambda ins: ins.then_inc(s_pp, 1)
                pe.wait_ge(s_ident, 1)
                pe.wait_ge(s_rows, 16 * 10)
                turn(ps[:, 0, 0:NR], rows[:], ident[0:NR, 0:NR])
                pe.wait_ge(s_wqkv, 16 * 3)
                for i in range(3):
                    last = turn(ps[:, 0, (i + 1) * P:(i + 2) * P], w_qkv[:, i, :], ident[:])
                step(last)
                pe.wait_ge(s_pv, PV_COLS)
                step(mm(ps[:, 1, 0:P], w_qkvT[:, 0, :], w_qkvT[:, 1, :]))
                pe.wait_ge(s_wall, 16 * 17)
                wv_t = w_qkvT[:, 2, :]
                w1f = w1[:, 1, :, :].rearrange("p e r -> p (e r)")
                mm(ps[:, 2, :], wv_t, w1f[:, 0:512])
                mm(ps[:, 3, 0:256], wv_t, w1f[:, 512:768])
                mm(ps[:, 3, 256:256 + P], wv_t, gw1[:, 1, :])
                step(mm(ps[:, 3, 384:384 + E], wv_t, rw[:, 1, :]))
                for k in range(4):
                    turn(ps[:, 4, k * P:(k + 1) * P], w2[:, k, :], ident[:])
                for k in range(2):
                    last = turn(ps[:, 5, k * P:(k + 1) * P], w2[:, 4 + k, :], ident[:])
                step(last)
                cond = cols[:, R_COND:R_COND + B]
                for z in range(NZ):
                    lhsT = gw1[:, 2, :] if z == NZ - 1 else w1[:, 2, z // RC, z % RC * P:(z % RC + 1) * P]
                    mm(ps[:, 6, z * B:(z + 1) * B], lhsT, cond)
                mm(ps[0:E, 6, 32:32 + B], rw[:, 2, :], cond)
                pe.wait_ge(s_pv, PV_SILU)
                for k, w in enumerate((wssq, wssk)):
                    for j in range(2):
                        last = mm(ps[:, 6, 64 + (2 * k + j) * B:64 + (2 * k + j + 1) * B], w[:, j * P:(j + 1) * P],
                                  silu_c[:])
                step(last)
                pe.wait_ge(s_pv, PV_SPREAD)
                for e in range(E):
                    mm(ps[:, 7, e * P:(e + 1) * P], spread[:, e, :], ow[:], stop=False)
                    mm(ps[:, 7, e * P:(e + 1) * P], ones[0:1, :], vec_row[:, 0, :], start=False)
                mm(ps[:, 7, E * P:], spread[:, E, :], wp1[:], stop=False)
                step(mm(ps[:, 7, E * P:], ones[0:1, :], vec_row[:, 1, :], start=False))
                pe.wait_ge(s_pv, PV_W2T)
                for k in range(E * RC):
                    last = mm(ps[:, k // 4, k % 4 * P:(k % 4 + 1) * P], w2T[:, k, :], ow[:])
                step(last)

            def before(b):
                def begin(name):
                    room(pe, b, name)
                    return bank(name)

                o = begin("ctxT")
                need(pe, s_c, 16 * (b + 1))
                for c in range(SC):
                    last = turn(o[:, c * P:(c + 1) * P], c_sb[:, c, :], ident[:])
                filled("ctxT", last)
                o = begin("nxT")
                need(pe, s_xn, b + 1)
                for t in range(TC):
                    last = turn(o[:, t * P:(t + 1) * P], xn[:, t, :], ident[:])
                filled("nxT", last)
                o = begin("qm")
                done(pe, b, "nxT")
                filled("qm", mm(o[:, 0:T], m_qk[:], nxT[:]))
                done(pe, b, "ctxT")
                done(pe, b, "qm")
                for t in range(TC):
                    o = begin(f"s0_{t}")
                    filled(f"s0_{t}", mm(o, qmT[:, t * P:(t + 1) * P], ctxT[:]))
                o = begin("hkvT")
                need(pe, s_cn, b + 1)
                for c in range(SC):
                    last = turn(o[:, c * P:(c + 1) * P], cn[:, c, :], ident[:])
                filled("hkvT", last)
                o = begin("kproj")
                done(pe, b, "hkvT")
                filled("kproj", mm(o, wkv1[:, 0:P], xkvT[:]))
                for t in range(TC):
                    o = begin(f"p0T_{t}")
                    need(pe, s_p0, TC * b + t + 1)
                    for c in range(SC):
                        last = turn(o[:, c * P:(c + 1) * P], p0[:, t, c * P:(c + 1) * P], ident[:])
                    filled(f"p0T_{t}", last)
                o = begin("vproj")
                for c in range(SC):
                    last = mm(o[:, c * P:(c + 1) * P], xkvT[:, c * P:(c + 1) * P], wkv1[:, P:2 * P])
                filled("vproj", last)
                o = begin("pc")
                done(pe, b, "p0T_0")
                done(pe, b, "p0T_1")
                for c in range(SC):
                    last = mm(o[:, 0:T], c_sb[:, c, :], p0T[:, c, :], start=(c == 0), stop=(c == SC - 1))
                filled("pc", last)
                for k in range(4):
                    name = f"hid_{k}"
                    o = begin(name)
                    if k == 0:
                        done(pe, b, "pc")
                    for j in range(2):
                        z = 2 * k + j
                        if z < NZ - 1:
                            wa, wb = w1[:, 0, z // RC, z % RC * P:(z % RC + 1) * P], w1ev[:, z * P:(z + 1) * P]
                            oz = o[:, j * T:(j + 1) * T]
                        elif z == NZ - 1:
                            wa, wb, oz = gw1[:, 0, :], gw1ev[:], o[:, 0:T]
                        else:
                            wa, wb, oz = rw[:, 0, :], rwev[:], o[0:E, T:2 * T]
                        mm(oz, wa, nxT[:], stop=False)
                        last = mm(oz, wb, pcT[:], start=False)
                    filled(name, last)
                o = begin("lgT")
                done(pe, b, "hid_3")
                pe.sem_inc(s_tick, 1)
                for t in range(TC):
                    last = turn(o[:, t * E:(t + 1) * E], lg[:, t * P:(t + 1) * P], ident[0:E, 0:E])
                filled("lgT", last)
                for t in range(TC):
                    name = f"eo_{t}"
                    o = begin(name)
                    for e in range(E):
                        for k in range(RC):
                            mm(o[:, e * P:(e + 1) * P], hT[:, e * RC + k, t * P:(t + 1) * P], w2o[:, e * RC + k, :],
                               start=(k == 0), stop=(k == RC - 1))
                    filled(name, mm(o[:, E * P:], hT[:, NZ - 1, t * P:(t + 1) * P], gw2[:]))
                o = begin("xqT")
                need(pe, s_xn1, b + 1)
                for t in range(TC):
                    last = turn(o[:, t * P:(t + 1) * P], xn1[:, t, :], ident[:])
                filled("xqT", last)
                o = begin("qproj")
                done(pe, b, "xqT")
                filled("qproj", mm(o[:, 0:T], wq1[:], xqT[:]))

            def maxima(b):
                for half in range(2):
                    need(pe, s_st[half], (b + 1) * ST_DMAS * 16)
                need(pe, s_pe, NH * b)
                for k in range(GM):
                    h, t = divmod(k, TC)
                    need(pe, s_gr, b * (GM + 1) + max(k - 3, 0))
                    mm(ps[:, k % 4, :], q_st[0:KR, h, t * P:(t + 1) * P], k_st[0:KR, h, :]).then_inc(s_gm, 1)
                need(pe, s_mp, b + 1)
                need(pe, s_gr, b * (GM + 1) + GM, hold=True)
                for t in range(TC):
                    last = turn(ps[0:NP * NH, 0, :].bitcast(BF16)[:, t * P:(t + 1) * P],
                                mparts[:, t, :, :].rearrange("p i h -> p (i h)"), identb[:])
                last.then_inc(s_gm, 1)

            def scores(b, h):
                if h == 0:
                    need(pe, s_mrow, 16 * (b + 1))
                need(pe, s_pe, NH * b + h - 1)
                for c in range(SC):
                    o = ps[:, 2 * (h % 2) + c // 2, c % 2 * T:(c % 2 + 1) * T]
                    last = mm(o, k_st[:, h, c * P:(c + 1) * P], q_st[:, h, :])
                last.then_inc(s_sc, 1)

            def outputs(b, g):
                if g == 0:
                    need(pe, s_vt, b + 1)
                need(pe, s_pe, NH * b + (g + 1) * GH)
                need(pe, s_od[g % 2], 4 * b + g // 2)
                for c in range(SC):
                    for j in range(GH):
                        last = mm(ps[j * QT:(j + 1) * QT, OB + g % 2, 0:T], vtile[:, c, g * GH + j, :],
                                  probs[:, g % 2, j, c * T:(c + 1) * T], start=(c == 0), stop=(c == SC - 1))
                last.then_inc(s_o, 1)

            def heads(b):
                for h in range(NH):
                    scores(b, h)
                    if h >= GH + 1 and (h - GH - 1) % GH == 0:
                        outputs(b, (h - GH - 1) // GH)
                outputs(b, NG - 1)

            def after(b):
                for t in range(TC):
                    need(pe, s_od[t], 4 * b + 2)
                    if t == 0:
                        need(pe, s_od[1], 4 * b + 2)
                    for g in range(NG):
                        last = turn(ps[:, OB + t, g * P:(g + 1) * P], o_sb[:, g, t * P:(t + 1) * P], ident[:])
                    last.then_inc(s_post, 1)
                for t in range(TC):
                    need(pe, s_od[t], 4 * b + 3)
                for t in range(TC):
                    last = turn(ps[:, OB, t * P:(t + 1) * P], on[:, t, :], ident[:])
                last.then_inc(s_post, 1)
                need(pe, s_od[0], 4 * b + 4)
                for t in range(TC):
                    last = mm(ps[:, OB + 1, t * P:(t + 1) * P], onT[:, t * P:(t + 1) * P], wp1[:])
                last.then_inc(s_post, 1)

            prepare()
            pe.wait_ge(s_pv, PV_ALL)
            before(0)
            pe.wait_ge(s_ones, 16)
            with pe.Fori(0, B - 1) as i:
                maxima(i)
                heads(i)
                before(i + 1)
                after(i)
            maxima(B - 1)
            heads(B - 1)
            after(B - 1)

        @block.vector
        def _(dve):
            V = nc.vector

            def prepare():
                prep = Chain(dve, s_pv, PV_ALL)
                prep.begin(0)
                dve.wait_ge(s_pp, 1)
                V.tensor_copy(cols[:], ps[:, 0, 0:NR])
                prep.step(V.tensor_copy(w_qkvT[:].rearrange("p a n -> p (a n)"), ps[:, 0, P:]))
                assert prep.n == PV_COLS
                dve.wait_ge(s_pp, 2)
                V.tensor_scalar(m_qk[:], ps[:, 1, 0:P], SCALE0, None, ALU.mult)
                dve.wait_ge(s_ps, 1)
                prep.wait()
                prep.link(V.scalar_tensor_tensor(silu_c[:], silu_t[:], 1.0, cols[:, R_COND:R_COND + B],
                                                 ALU.add, ALU.mult))
                prep.step(V.tensor_scalar(silu_c[:], silu_c[:], 0.5, None, ALU.mult))
                assert prep.n == PV_SILU
                dve.wait_ge(s_const, 1)
                for e in range(E):
                    V.tensor_scalar(spread[:, e, :], ones[:], cols[:, R_EB2 + e:R_EB2 + e + 1], None, ALU.mult)
                prep.step(V.tensor_scalar(spread[:, E, :], ones[:], cols[:, R_BV:R_BV + 1], None, ALU.mult))
                dve.wait_ge(s_pp, 3)
                V.tensor_copy(w1ev[:, 0:512], ps[:, 2, :])
                V.tensor_copy(w1ev[:, 512:768], ps[:, 3, 0:256])
                V.tensor_copy(gw1ev[:], ps[:, 3, 256:384])
                V.tensor_copy(rwev[:], ps[:, 3, 384:384 + E])
                dve.wait_ge(s_pp, 4)
                V.tensor_copy(w2T[:, 0:4, :].rearrange("p a n -> p (a n)"), ps[:, 4, :])
                prep.step(V.tensor_copy(w2T[:, 4:6, :].rearrange("p a n -> p (a n)"), ps[:, 5, 0:256]))
                assert prep.n == PV_W2T
                dve.wait_ge(s_pp, 5)
                V.tensor_tensor(allv[:, :, V_Z:V_Z + NZ].rearrange("p b z -> p z b"),
                                ps[:, 6, 0:NZ * B].rearrange("p (z b) -> p z b", b=B),
                                cols[:, R_B1:R_B1 + NZ].unsqueeze(2).to_broadcast([P, NZ, B]), ALU.add)
                V.tensor_tensor(allv[:, :, V_ADA:V_ADA + 4].rearrange("p b z -> p z b"),
                                ps[:, 6, 64:64 + 4 * B].rearrange("p (z b) -> p z b", b=B),
                                cols[:, R_SSQ:R_SSQ + 4].unsqueeze(2).to_broadcast([P, 4, B]), ALU.add)
                prep.link(V.tensor_scalar(rball[:], ps[0:E, 6, 32:32 + B], rb[:, 0:1], None, ALU.add))
                V.tensor_scalar(allv[:, :, V_HALF:V_HALF + NZ], allv[:, :, V_Z:V_Z + NZ], 0.5, None, ALU.mult)
                for k in range(2):
                    z = V_ADA + 2 * k
                    prep.step(V.tensor_scalar(allv[:, :, z:z + 1], allv[:, :, z:z + 1], 1.0, None, ALU.add))
                dve.wait_ge(s_pp, 6)
                V.tensor_copy(bias2[:].rearrange("p a n -> p (a n)"), ps[:, 7, 0:E * P])
                V.tensor_copy(bias_o[:], ps[:, 7, E * P:])
                dve.wait_ge(s_pp, 7)
                V.tensor_copy(w2o[:, 0:4, :].rearrange("p a n -> p (a n)"), ps[:, 0, :])
                prep.link(V.tensor_copy(w2o[:, 4:6, :].rearrange("p a n -> p (a n)"), ps[:, 1, 0:256]))
                prep.end()

            own = Chain(dve, s_cv, 22)
            late = Chain(dve, s_cm, 2)

            def before(b):
                own.begin(b)
                need(dve, s_x, 16 * (b + 1))
                for t in range(TC):
                    V.bn_stats(stats[:, t, :], x_sb[:, t, :])
                need(dve, s_c, 16 * (b + 1))
                for c in range(SC):
                    last = V.bn_stats(stats[:, TC + c, :], c_sb[:, c, :])
                own.link(last)
                at_b = slice(b, b + 1) if isinstance(b, int) else bass.ds(b, 1)
                V.tensor_copy(rcur[:], rball[:, at_b])
                for t in range(TC + SC):
                    last = V.bn_aggr(mv[:, t, :], stats[:, t, :])
                V.tensor_copy(cur[:], allv[:, at_b, :].rearrange("p a v -> p (a v)"))
                own.link(last)
                V.tensor_scalar(ve[:], mv[:, :, 1], EPS, None, ALU.add).then_inc(s_var, 1)
                need(dve, s_rstd, 2 * b + 1)
                for t in range(TC):
                    last = V.tensor_scalar(xn[:, t, :], x_sb[:, t, :], mv[:, t, 0:1], rstd[:, t:t + 1],
                                           ALU.subtract, ALU.mult)
                last.then_inc(s_xn, 1)
                for c in range(SC):
                    last = V.tensor_scalar(cn[:, c, :], c_sb[:, c, :], mv[:, TC + c, 0:1],
                                           rstd[:, TC + c:TC + c + 1], ALU.subtract, ALU.mult)
                last.then_inc(s_cn, 1)
                full(dve, b, "nxT")
                emptied("nxT", V.tensor_scalar(nxT[:], bank("nxT")[:, 0:T], cols[:, R_GAMMA:R_GAMMA + 1],
                                               cols[:, R_BETA:R_BETA + 1], ALU.mult, ALU.add))
                full(dve, b, "qm")
                emptied("qm", V.tensor_copy(qmT[:], bank("qm")[:, 0:T]))
                for t in range(TC):
                    full(dve, b, f"s0_{t}")
                    V.tensor_reduce(nm0[:, t:t + 1], bank(f"s0_{t}"), AX_X, ALU.max, negate=True).then_inc(s_nm0, 1)
                full(dve, b, "hkvT")
                emptied("hkvT", V.tensor_scalar(xkvT[:], bank("hkvT"), cur[:, V_ADA + 2:V_ADA + 3],
                                                cur[:, V_ADA + 3:V_ADA + 4], ALU.mult, ALU.add))
                for t in range(TC):
                    done(dve, b, f"s0_{t}")
                    own.link(V.reciprocal(rs0[:, t:t + 1], sum0[:, t:t + 1]))
                    V.tensor_scalar(p0[:, t, :], p0[:, t, :], rs0[:, t:t + 1], None, ALU.mult).then_inc(s_p0, 1)
                full(dve, b, "kproj")
                need(dve, s_kp, b) if not (isinstance(b, int) and b == 0) else None
                emptied("kproj", V.tensor_scalar(kf[:], bank("kproj"), cols[:, R_BK:R_BK + 1], None, ALU.add))
                full(dve, b, "p0T_1")
                emptied("p0T_1", V.tensor_copy(p0T[:, :, P:T], bank("p0T_1").rearrange("p (c t) -> p c t", c=SC)))
                full(dve, b, "pc")
                emptied("pc", V.tensor_copy(pcT[:], bank("pc")[:, 0:T]))
                for k in range(4):
                    name = f"hid_{k}"
                    need(dve, s_sg, 4 * b + k + 1)
                    for j in range(min(2, NZ - 2 * k)):
                        z = 2 * k + j
                        last = V.scalar_tensor_tensor(hT[:, z, :], bank(name)[:, j * T:(j + 1) * T],
                                                      cur[:, V_Z + z:V_Z + z + 1], tz[:, z, :], ALU.add, ALU.mult)
                    if k == 3:
                        last = V.tensor_scalar(lg[:], bank(name)[0:E, T:2 * T], rcur[:, 0:1], None, ALU.add)
                    emptied(name, last)
                full(dve, b, "lgT")
                lgT = bank("lgT")[:, 0:TC * E].rearrange("p (t e) -> p t e", e=E)
                own.link(V.tensor_reduce(rmx[:], lgT, AX_X, ALU.max))
                own.step(V.tensor_tensor(rd[:], lgT, rmx[:].unsqueeze(2).to_broadcast([P, TC, E]), ALU.subtract))
                own.wait()
                dve.sem_inc(s_rd, 1)
                need(dve, s_re, b + 1)
                own.link(V.tensor_reduce(rsum[:], re[:], AX_X, ALU.add))
                own.link(V.reciprocal(rinv[:], rsum[:]))
                emptied("lgT", V.tensor_tensor(pr[:], re[:], rinv[:].unsqueeze(2).to_broadcast([P, TC, E]), ALU.mult))
                done(dve, b, "lgT")
                dve.sem_inc(s_pr, 1)
                need(dve, s_pb, b + 1)
                for t in range(TC):
                    name = f"eo_{t}"
                    o = bank(name)
                    full(dve, b, name)
                    for e in range(E):
                        prev = pb[:, t, :] if e == 0 else yacc[:, e - 1, t, :]
                        own.link(V.scalar_tensor_tensor(yacc[:, e, t, :], o[:, e * P:(e + 1) * P],
                                                        pr[:, t, e:e + 1], prev, ALU.mult, ALU.add))
                    emptied(name, V.tensor_tensor(zg[:, t, :], o[:, E * P:], bias_g[:], ALU.add))
                for t in range(TC):
                    done(dve, b, f"eo_{t}")
                dve.sem_inc(s_zg, 1)
                need(dve, s_tg, b + 1)
                own.link(V.scalar_tensor_tensor(ug[:], tg[:], 1.0, yacc[:, E - 1, :, :], ALU.add, ALU.mult))
                need(dve, s_res, b)
                own.link(V.scalar_tensor_tensor(x1[:], ug[:], 0.5, x_sb[:], ALU.mult, ALU.add))
                dve.sem_inc(s_x1, 1)
                for t in range(TC):
                    last = V.bn_stats(st1[:, t, :], x1[:, t, :])
                own.link(last)
                V.tensor_copy(rmx[:], rinv[:])
                for t in range(TC):
                    last = V.bn_aggr(mv1[:, t, :], st1[:, t, :])
                own.link(last)
                V.tensor_scalar(ve1[:], mv1[:, :, 1], EPS, None, ALU.add).then_inc(s_var, 1)
                need(dve, s_rstd, 2 * b + 2)
                for t in range(TC):
                    last = V.tensor_scalar(xn1[:, t, :], x1[:, t, :], mv1[:, t, 0:1], rstd1[:, t:t + 1],
                                           ALU.subtract, ALU.mult)
                last.then_inc(s_xn1, 1)
                full(dve, b, "xqT")
                emptied("xqT", V.tensor_scalar(xqT[:], bank("xqT")[:, 0:T], cur[:, V_ADA:V_ADA + 1],
                                               cur[:, V_ADA + 1:V_ADA + 2], ALU.mult, ALU.add))
                full(dve, b, "qproj")
                emptied("qproj", V.tensor_scalar(qf[:], bank("qproj")[:, 0:T], cols[:, R_BQ:R_BQ + 1], SCALE1,
                                                 ALU.add, ALU.mult))
                done(dve, b, "qproj")
                need(dve, s_qscr, b * NP * 16)
                own.link(V.tensor_copy(qp[:, 0, :], qf[:]))
                own.link(V.tensor_tensor(qr[:, 0, :], qf[:], qp[:, 0, :], ALU.subtract))
                own.link(V.tensor_copy(qp[:, 1, :], qr[:, 0, :]))
                own.link(V.tensor_tensor(qr[:, 1, :], qr[:, 0, :], qp[:, 1, :], ALU.subtract))
                V.tensor_copy(qp[:, 2, :], qr[:, 1, :]).then_inc(s_qp, 1)
                own.end()

            top = Chain(dve, s_cx, 4)

            def maxima(b):
                top.begin(b)
                for k in range(GM):
                    h, t = divmod(k, TC)
                    need(dve, s_gm, b * (GM + 1) + k + 1)
                    V.tensor_reduce(mx[:, t, h:h + 1], ps[:, k % 4, :], AX_X, ALU.max, negate=True)\
                        .then_inc(s_gr, 1)
                need(dve, s_gr, b * (GM + 1) + GM)
                top.link(V.tensor_copy(mparts[:, :, 0, :], mx[:]))
                top.link(V.tensor_tensor(mr[:, 0], mx[:], mparts[:, :, 0, :], ALU.subtract))
                top.link(V.tensor_copy(mparts[:, :, 1, :], mr[:, 0]))
                top.link(V.tensor_tensor(mr[:, 1], mr[:, 0], mparts[:, :, 1, :], ALU.subtract))
                V.tensor_copy(mparts[:, :, 2, :], mr[:, 1]).then_inc(s_mp, 1)
                need(dve, s_gm, (b + 1) * (GM + 1))
                V.tensor_copy(mT[:], ps[0:NP * NH, 0, :].bitcast(BF16)[:, 0:T]).then_inc(s_gr, 1)
                top.end()

            def outputs(b, g):
                need(dve, s_o, NG * b + g + 1)
                V.tensor_copy(o_sb[:, g, :], ps[:, OB + g % 2, 0:T]).then_inc(s_od[g % 2], 1)

            def after(b):
                late.begin(b)
                for t in range(TC):
                    o = ps[:, OB + t, :].rearrange("p (h q) -> p h q", q=QT)
                    need(dve, s_post, 4 * b + t + 1)
                    late.link(V.reciprocal(rs1[:, t, :], o[:, :, DH]))
                    V.tensor_tensor(on[:, t, :].rearrange("p (h d) -> p h d", d=DH), o[:, :, 0:DH],
                                    rs1[:, t, :].unsqueeze(2).to_broadcast([P, NH, DH]), ALU.mult)\
                        .then_inc(s_od[t], 1)
                need(dve, s_post, 4 * b + 3)
                V.tensor_copy(onT[:], ps[:, OB, 0:T]).then_inc(s_od[0], 1)
                need(dve, s_post, 4 * b + 4)
                need(dve, s_res, b + 1)
                need(dve, s_out, 16 * b)
                V.tensor_tensor(y_sb[:], ps[:, OB + 1, 0:T].rearrange("p (t d) -> p t d", d=P), resid[:], ALU.add)\
                    .then_inc(s_od[1], 1)
                need(dve, s_od[1], 4 * b + 4)
                dve.sem_inc(s_y, 1)
                late.end()

            prepare()
            before(0)
            with dve.Fori(0, B - 1) as i:
                maxima(i)
                for g in range(NG):
                    outputs(i, g)
                before(i + 1)
                after(i)
            maxima(B - 1)
            for g in range(NG):
                outputs(B - 1, g)
            after(B - 1)


_INS = [
    "x", "cond_1024", "ctx_1024", "L0_xcond_ln_gamma", "L0_xcond_ln_beta", "L0_xcond_Wq", "L0_xcond_Wk",
    "L0_xcond_Wv", "L0_xcond_router_W", "L0_xcond_router_b", "L0_xcond_e_w1", "L0_xcond_e_b1", "L0_xcond_e_w2",
    "L0_xcond_e_b2", "L0_xcond_gate_w1", "L0_xcond_gate_b1", "L0_xcond_gate_w2", "L0_xcond_gate_b2",
    "L0_xcond_out_w", "L0_xcond_out_b", "L1_xcond_Wq", "L1_xcond_bq", "L1_xcond_Wkv", "L1_xcond_bkv",
    "L1_xcond_Wp", "L1_xcond_bp", "L1_xcond_Wss_q", "L1_xcond_bss_q", "L1_xcond_Wss_kv", "L1_xcond_bss_kv",
]


def kernel(**inputs):
    import numpy as _np
    import concourse.bacc as _bacc
    from concourse import mybir as _mybir
    from concourse.bass_utils import run_bass_kernel_spmd as _run

    nc = _bacc.Bacc("TRN2", target_bir_lowering=False, num_devices=1)
    arrays, aps = {}, {}
    for name in _INS:
        array = _np.ascontiguousarray(inputs[name])
        arrays[f"in_{name}"] = array
        aps[name] = nc.dram_tensor(f"in_{name}", array.shape, _mybir.dt.from_np(array.dtype),
                                   kind="ExternalInput").ap()
    out = nc.dram_tensor("out_0", (B, T, P), _mybir.dt.float32, kind="ExternalOutput").ap()
    build(nc, aps, out)
    r = _run(nc, [arrays], core_ids=[0])
    return r.results[0]["out_0"]
```

```python
from contextlib import ExitStack

import concourse.bass as bass
from concourse import mybir

F32 = mybir.dt.float32
BF16 = mybir.dt.bfloat16
ACT = mybir.ActivationFunctionType
ALU = mybir.AluOpType
AX_X = mybir.AxisListType.X

P = 128
B = 4
T, TC = 256, 2
S, SC = 512, 4
E, RC = 3, 2
NH, DH = 16, 8
GH = 4
NG = NH // GH
PV_COLS, PV_SILU, PV_SPREAD, PV_W2T, PV_ALL = 1, 3, 4, 5, 9
QT = 32
NZ = E * RC + 1
NP = 3
KR = NP * NP * DH
EPS = 1e-5
SCALE0 = float(P) ** -0.5
SCALE1 = float(DH) ** -0.5

R_B1, R_GB1, R_GAMMA, R_BETA, R_BQ, R_BK, R_BV, R_SSQ, R_SSK, R_COND, R_EB2 = 0, 6, 7, 8, 9, 10, 11, 12, 14, 16, 20
NR = 23
V_Z, V_HALF, V_ADA, NV = 0, NZ, 2 * NZ, 2 * NZ + 4

SPARE = ["ctxT", "nxT", "qm", "s0_0", "s0_1", "hkvT", "kproj", "p0T_0", "p0T_1", "vproj", "pc",
         "hid_0", "hid_1", "hid_2", "hid_3", "lgT", "eo_0", "eo_1", "xqT", "qproj"]
HALF = len(SPARE) // 2
MHALF = NG * (GH * TC + 1) // 2
NU = 2 * NH

STAGES = ["start", "ctxT", "nxT", "qm", "s0", "hkvT", "kproj", "p0T", "vproj", "pc", "hid_0", "hid_1", "act_0",
          "hid_2", "act_1", "hid_3", "act_2", "act_3", "lgT", "eo", "x1", "xqT", "qproj"]

def maxima_of_groups(g):
    first, second = [("tile", (g, k)) for k in range(GH * TC)], [("tile", (g + 1, k)) for k in range(GH * TC)]
    return first + second[:1] + [("rows", g)] + second[1:] + [("rows", g + 1)]


MAXIMA = maxima_of_groups(0) + maxima_of_groups(2)


def merged(*lists):
    keyed = [((n + 0.5) / len(items), m, n, item) for m, items in enumerate(lists) for n, item in enumerate(items)]
    return [item for _, _, _, item in sorted(keyed, key=lambda k: k[:3])]


def schedule():
    heads = []
    for u in range(NU):
        heads.append(("this", "unit", u))
        if u % (2 * GH) == 1 and u > 1:
            heads.append(("this", "pv", u // (2 * GH) - 1))
    heads.append(("this", "pv", NG - 1))
    stages = [("next", "stage", name) for name in STAGES]
    late_maxima = [("this", *m) for m in maxima_of_groups(2)]
    early_maxima = [("next", *m) for m in maxima_of_groups(0)]
    after = [("this", "after", n) for n in range(4)]
    dma_k, dma_q = [("next", "k_rows", 0)], [("next", "q_rows", 0)]
    cut = CUT
    return ([("this", "values", 0)] + merged(stages, heads[:cut], late_maxima) + dma_k + dma_q
            + [("next", "load_ahead", 0)] + heads[cut:] + merged(early_maxima, after)
            + [("next", "resid", 0), ("this", "store", 0)])


CUT = 22
ORDER = schedule()
FIRST = [o for o in ORDER if o[0] == "next"]
LAST = [o for o in ORDER if o[0] == "this"]


def walk(shares, order, this, following):
    for whose, kind, which in order:
        if kind in shares:
            shares[kind](this if whose == "this" else following, which)


HIDDEN = [f"hid_{k}" for k in range(4)]
ACTIVATED = [f"act_{k}" for k in range(4)]


def spare_bank(name):
    return SPARE.index(name) % 2


CREDIT = 16


class Chain:

    def __init__(self, eng, sem, per):
        self.eng, self.sem, self.per = eng, sem, per

    def begin(self, b):
        self.base, self.n = b * self.per, 0

    def step(self, ins):
        self.n += 1
        ins.then_inc(self.sem, 1)

    def link(self, ins):
        self.step(ins)
        self.wait()

    def wait(self):
        self.eng.wait_ge(self.sem, self.base + self.n)

    def end(self):
        assert self.n == self.per, (self.n, self.per)


def build(nc, a, out):
    with ExitStack() as ctx:
        def sb(name, shape, dt=F32):
            return ctx.enter_context(nc.sbuf_tensor(name, shape, dt))

        def sem(name):
            return ctx.enter_context(nc.semaphore(name))

        vec_rows = sb("vec_rows", [NR, P])
        cols = sb("cols", [P, NR])
        w_qkv = sb("w_qkv", [P, 3, P])
        w_qkvT = sb("w_qkvT", [P, 3, P])
        w1 = sb("w1", [P, 3, E, RC * P])
        gw1 = sb("gw1", [P, 3, P])
        rw = sb("rw", [P, 3, E])
        rb = sb("rb", [E, 1])
        w2 = sb("w2", [P, E * RC, P])
        w2T = sb("w2T", [P, E * RC, P])
        gw2 = sb("gw2", [P, P])
        ow = sb("ow", [P, P])
        wq1 = sb("wq1", [P, P])
        wkv1 = sb("wkv1", [P, 2 * P])
        wp1 = sb("wp1", [P, P])
        wssq = sb("wssq", [P, 2 * P])
        wssk = sb("wssk", [P, 2 * P])
        m_qk = sb("m_qk", [P, P])
        w1ev = sb("w1ev", [P, E * RC * P])
        gw1ev = sb("gw1ev", [P, P])
        rwev = sb("rwev", [P, E])
        w2o = sb("w2o", [P, E * RC, P])
        bias2 = sb("bias2", [P, E, P])
        bias_g = sb("bias_g", [P, P])
        bias_o = sb("bias_o", [P, P])
        vec_row = sb("vec_row", [1, 2, P])
        ones = sb("ones", [P, P])
        spread = sb("spread", [P, E + 1, P])
        silu_t = sb("silu_t", [P, B])
        silu_c = sb("silu_c", [P, B])
        ident = sb("ident", [P, P])
        identb = sb("identb", [P, P], BF16)
        onesb = sb("onesb", [NP * NH * S // T, T], BF16)
        allv = sb("allv", [P, B, NV])
        rball = sb("rball", [E, B])
        cur = sb("cur", [P, NV])
        rcur = sb("rcur", [E, 1])
        mhalf = sb("mhalf", [P, TC + SC])

        x_sb = sb("x_sb", [P, TC, P])
        c_sb = sb("c_sb", [P, SC, P])
        stats = sb("stats", [P, TC + SC, 6])
        mv = sb("mv", [P, TC + SC, 2])
        ve = sb("ve", [P, TC + SC])
        rstd = sb("rstd", [P, TC + SC])
        xn = sb("xn", [P, TC, P])
        cn = sb("cn", [P, SC, P])
        ctxT = sb("ctxT", [P, S])
        nxT = sb("nxT", [P, T])
        qmT = sb("qmT", [P, T])
        nm0 = sb("nm0", [P, TC])
        sum0 = sb("sum0", [P, TC])
        rs0 = sb("rs0", [P, TC])
        p0 = sb("p0", [P, TC, S])
        p0T = sb("p0T", [P, SC, T])
        pcT = sb("pcT", [P, T])
        tz = sb("tz", [P, 8, T])
        hT = sb("hT", [P, 8, T])
        lg = sb("lg", [E, T])
        rmx = sb("rmx", [P, TC])
        rd = sb("rd", [P, TC, E])
        re = sb("re", [P, TC, E])
        rsum = sb("rsum", [P, TC])
        rinv = sb("rinv", [P, TC])
        pr = sb("pr", [P, TC, E])
        pbt = sb("pbt", [P, TC, E, P])
        pbs = sb("pbs", [P, TC, P])
        pb = sb("pb", [P, TC, P])
        yacc = sb("yacc", [P, 3, TC, P])
        zg = sb("zg", [P, TC, P])
        tg = sb("tg", [P, TC, P])
        ug = sb("ug", [P, TC, P])
        x1 = sb("x1", [P, TC, P])
        st1 = sb("st1", [P, TC, 6])
        mv1 = sb("mv1", [P, TC, 2])
        ve1 = sb("ve1", [P, TC])
        rstd1 = sb("rstd1", [P, TC])
        xn1 = sb("xn1", [P, TC, P])
        resid = sb("resid", [P, TC, P])
        xkvT = sb("xkvT", [P, S])
        xqT = sb("xqT", [P, T])
        kf = sb("kf", [P, S])
        kr = sb("kr", [P, 2, S])
        kp = sb("kp", [P, NP, S], BF16)
        qf = sb("qf", [P, T])
        qr = sb("qr", [P, 2, T])
        qp = sb("qp", [P, NP, T], BF16)
        vst = sb("vst", [P, SC, P])
        vtile = sb("vtile", [P, SC, NH, QT])
        q_st = sb("q_st", [P, NH, T], BF16)
        k_st = sb("k_st", [P, NH, S], BF16)
        probs = sb("probs", [P, 2, GH, SC * T])
        o_sb = sb("o_sb", [P, NG, T])
        rs1 = sb("rs1", [P, TC, NH])
        on = sb("on", [P, TC, P])
        onT = sb("onT", [P, T])
        y_sb = sb("y_sb", [P, TC, P])
        mx = sb("mx", [P, TC, NH])
        mr = sb("mr", [P, 2, TC, GH])
        mparts = sb("mparts", [P, TC, NP, GH], BF16)
        mT = sb("mT", [NP * GH, 2, T], BF16)

        ps = ctx.enter_context(nc.psum_tensor("ps", [P, 8, 512], F32))
        SB, XB, OB, MB = 0, 2, 4, 6

        q_scr = nc.dram_tensor("q_scr", (NP, DH, NH, T), BF16, kind="Internal").ap()
        k_scr = nc.dram_tensor("k_scr", (DH, NP, NH, S), BF16, kind="Internal").ap()

        s_rows = sem("s_rows")
        s_wqkv = sem("s_wqkv")
        s_wall = sem("s_wall")
        s_ident = sem("s_ident")
        s_const = sem("s_const")
        s_zero = sem("s_zero")
        s_ones = sem("s_ones")
        s_pp = sem("s_pp")
        s_pv = sem("s_pv")
        s_ps = sem("s_ps")
        s_x = sem("s_x")
        s_c = sem("s_c")
        s_var = sem("s_var")
        s_rstd = sem("s_rstd")
        s_xn = sem("s_xn")
        s_cn = sem("s_cn")
        s_full = [sem("s_full0"), sem("s_full1")]
        s_done = [sem("s_done0"), sem("s_done1")]
        s_nm0 = sem("s_nm0")
        s_p0 = sem("s_p0")
        s_tz = sem("s_tz")
        s_sg = sem("s_sg")
        s_rd = sem("s_rd")
        s_re = sem("s_re")
        s_pr = sem("s_pr")
        s_pb = sem("s_pb")
        s_zg = sem("s_zg")
        s_tg = sem("s_tg")
        s_x1 = sem("s_x1")
        s_xn1 = sem("s_xn1")
        s_res = sem("s_res")
        s_kp = sem("s_kp")
        s_qp = sem("s_qp")
        s_kscr = sem("s_kscr")
        s_qscr = sem("s_qscr")
        s_st = [sem("s_stA"), sem("s_stB")]
        s_vt = sem("s_vt")
        s_sc = sem("s_sc")
        s_pe = sem("s_pe")
        s_o = sem("s_o")
        s_od = [sem("s_od0"), sem("s_od1")]
        s_post = sem("s_post")
        s_y = sem("s_y")
        s_out = sem("s_out")
        s_xf = [sem("s_xf0"), sem("s_xf1")]
        s_xd = [sem("s_xd0"), sem("s_xd1")]
        s_mp = sem("s_mp")
        s_mrow = [sem("s_mrow0"), sem("s_mrow1")]
        s_cv = sem("s_cv")
        s_cm = sem("s_cm")
        s_cx = sem("s_cx")
        s_cc = sem("s_cc")
        s_cg = sem("s_cg")
        s_tick = sem("s_tick")

        free_again = [*s_done, s_o, *s_od, s_pe, s_y, s_x1, s_kscr, s_qscr, *s_st, s_sc, *s_xd, *s_mrow, s_res, s_vt, s_out]
        ST_DMAS = 2 * NP

        def need(eng, s, value, hold=False):
            if isinstance(value, int) and value <= 0:
                return
            if s in free_again:
                value = value + CREDIT
            eng.wait_ge(s, value)
            if hold:
                eng.sem_inc(s_tick, 1)

        def full(eng, b, name):
            k = SPARE.index(name)
            need(eng, s_full[k % 2], b * HALF + k // 2 + 1)

        def done(eng, b, name, hold=False):
            k = SPARE.index(name)
            need(eng, s_done[k % 2], b * HALF + k // 2 + 1, hold)

        def room(eng, b, name):
            k = SPARE.index(name)
            need(eng, s_done[k % 2], b * HALF + k // 2)

        def bank(name):
            return ps[:, MB + spare_bank(name), :]

        def filled(name, ins):
            ins.then_inc(s_full[spare_bank(name)], 1)

        def emptied(name, ins):
            ins.then_inc(s_done[spare_bank(name)], 1)

        block = ctx.enter_context(nc.Block())

        @block.sync
        def _(sp):
            def v(name, r):
                return a[name].rearrange("(r d) -> r d", r=r)

            def at(t, b):
                return t[b:b + 1] if isinstance(b, int) else t[bass.ds(b, 1)]

            def waits(*pairs):
                for s, x in pairs:
                    need(sp, s, x, hold=not isinstance(x, int))

            def load_batch(b):
                waits((s_x1, b))
                sp.dma_start(x_sb[:], at(a["x"].rearrange("b (c p) d -> b p c d", p=P), b)).then_inc(s_x, 16)
                sp.dma_start(c_sb[:], at(a["ctx_1024"].rearrange("b (c p) d -> b p c d", p=P), b)).then_inc(s_c, 16)

            def k_rows(b, _):
                waits((s_kp, b + 1), (s_st[0], b * ST_DMAS * 16), (s_st[1], b * ST_DMAS * 16))
                for i in range(NP):
                    sp.dma_start(k_scr[:, i, :, :].rearrange("d h t -> h d t"), kp[:, i, :]).then_inc(s_kscr, 16)

            def q_rows(b, _):
                waits((s_qp, b + 1))
                for i in range(NP):
                    sp.dma_start(q_scr[i].rearrange("d h t -> h d t"), qp[:, i, :]).then_inc(s_qscr, 16)
                for half in range(2):
                    h0, h1 = half * NH // 2, (half + 1) * NH // 2
                    waits((s_kscr, (b + 1) * NP * 16), (s_qscr, (b + 1) * NP * 16), (s_sc, (b - 1) * NU + 2 * h1))
                    for i in range(NP):
                        r = slice(i * NP * DH, (i + 1) * NP * DH)
                        sp.dma_start(k_st[r, h0:h1, :], k_scr[:, :, h0:h1, :]).then_inc(s_st[half], 16)
                        sp.dma_start(q_st[r, h0:h1, :],
                                     q_scr[i, :, h0:h1, :].rearrange("d h t -> d (h t)").unsqueeze(1)
                                     .to_broadcast([DH, NP, NH // 2 * T])).then_inc(s_st[half], 16)

            def rows(b, g):
                m = MAXIMA.index(("rows", g))
                waits((s_xd[m % 2], b * MHALF + m // 2 + 1), (s_sc, (b - 1) * NU + 2 * GH * (g + 1)))
                sp.dma_start(q_st[KR:KR + NP, g * GH:(g + 1) * GH, :], mT[:, g % 2, :]).then_inc(s_mrow[g % 2], 16)

            def store(b, _):
                waits((s_y, b + 1))
                sp.dma_start(at(out.rearrange("b (c p) d -> b p c d", p=P), b), y_sb[:]).then_inc(s_out, 16)

            def load_ahead(b, _):
                load_batch(b + 1)

            shares = dict(k_rows=k_rows, q_rows=q_rows, rows=rows, store=store)
            ahead = dict(shares, load_ahead=load_ahead)

            for i, name in enumerate(("L0_xcond_Wq", "L0_xcond_Wk", "L0_xcond_Wv")):
                sp.dma_start(w_qkv[:, i, :], a[name]).then_inc(s_wqkv, 16)
            load_batch(0)
            sp.dma_start(vec_rows[R_B1:R_B1 + E * RC, :],
                         a["L0_xcond_e_b1"].rearrange("e (k r) -> (e k) r", k=RC)).then_inc(s_rows, 16)
            for r, n, name in ((R_GB1, 1, "L0_xcond_gate_b1"), (R_GAMMA, 1, "L0_xcond_ln_gamma"),
                               (R_BETA, 1, "L0_xcond_ln_beta"), (R_BQ, 1, "L1_xcond_bq"), (R_BK, 2, "L1_xcond_bkv"),
                               (R_SSQ, 2, "L1_xcond_bss_q"), (R_SSK, 2, "L1_xcond_bss_kv")):
                sp.dma_start(vec_rows[r:r + n, :], v(name, n)).then_inc(s_rows, 16)
            sp.dma_start(vec_rows[R_COND:R_COND + B, :], a["cond_1024"]).then_inc(s_rows, 16)
            sp.dma_start(vec_rows[R_EB2:R_EB2 + E, :], a["L0_xcond_e_b2"]).then_inc(s_rows, 16)
            for k in range(3):
                sp.dma_start(w1[:, k, :, :], a["L0_xcond_e_w1"].rearrange("e (k c) r -> k c e r", k=3)[k])\
                    .then_inc(s_wall, 16)
            sp.dma_start(gw1[:], a["L0_xcond_gate_w1"].rearrange("(k c) r -> c k r", k=3)).then_inc(s_wall, 16)
            sp.dma_start(rw[:], a["L0_xcond_router_W"].rearrange("(k c) r -> c k r", k=3)).then_inc(s_wall, 16)
            sp.dma_start(w2[:], a["L0_xcond_e_w2"].rearrange("e (k r) h -> r (e k) h", k=RC)).then_inc(s_wall, 16)
            for t, name in ((gw2, "L0_xcond_gate_w2"), (ow, "L0_xcond_out_w"), (wq1, "L1_xcond_Wq"),
                            (wkv1, "L1_xcond_Wkv"), (wp1, "L1_xcond_Wp"), (wssq, "L1_xcond_Wss_q"),
                            (wssk, "L1_xcond_Wss_kv")):
                sp.dma_start(t[:], a[name]).then_inc(s_wall, 16)
            sp.dma_start(rb[:], v("L0_xcond_router_b", E)).then_inc(s_wall, 16)
            sp.dma_start(vec_row[:, 0, :], v("L0_xcond_out_b", 1)).then_inc(s_wall, 16)
            sp.dma_start(vec_row[:, 1, :], v("L1_xcond_bp", 1)).then_inc(s_wall, 16)
            sp.dma_start(bias_g[:], v("L0_xcond_gate_b2", 1).to_broadcast([P, P])).then_inc(s_wall, 16)
            sp.wait_ge(s_const, 1)
            sp.wait_ge(s_zero, 1)
            sp.dma_start(k_st[KR:KR + NP, :, :], onesb[:]).then_inc(s_ones, 16)
            walk(ahead, FIRST, None, 0)
            with sp.Fori(0, B - 2) as i:
                walk(ahead, ORDER, i, i + 1)
            walk(shares, ORDER, B - 2, B - 1)
            walk(shares, LAST, B - 1, None)
            need(sp, s_out, 16 * B)

        @block.gpsimd
        def _(pool):
            own = Chain(pool, s_cg, 8)

            def stage(b, name):
                if name == "start":
                    own.begin(b)
                    need(pool, s_var, 2 * b + 1)
                    nc.gpsimd.tensor_tensor(rstd[:], ve[:], mhalf[:], ALU.pow).then_inc(s_rstd, 1)
                elif name == "kproj":
                    need(pool, s_kscr, b * NP * 16, hold=True)
                    done(pool, b, "kproj", hold=True)
                    own.link(nc.gpsimd.tensor_copy(kp[:, 0, :], kf[:]))
                    own.link(nc.gpsimd.tensor_tensor(kr[:, 0, :], kf[:], kp[:, 0, :], ALU.subtract))
                    pool.sem_inc(s_tick, 1)
                    own.link(nc.gpsimd.tensor_copy(kp[:, 1, :], kr[:, 0, :]))
                    own.link(nc.gpsimd.tensor_tensor(kr[:, 1, :], kr[:, 0, :], kp[:, 1, :], ALU.subtract))
                    pool.sem_inc(s_tick, 1)
                    nc.gpsimd.tensor_copy(kp[:, 2, :], kr[:, 1, :]).then_inc(s_kp, 1)
                elif name in HIDDEN:
                    k = HIDDEN.index(name)
                    n = min(2, NZ - 2 * k)
                    need(pool, s_tz, 4 * b + k + 1, hold=True)
                    nc.gpsimd.tensor_scalar(tz[:, 2 * k:2 * k + n, :], tz[:, 2 * k:2 * k + n, :], 0.5, 0.5,
                                            ALU.mult, ALU.add).then_inc(s_sg, 1)
                elif name == "lgT":
                    need(pool, s_pr, b + 1, hold=True)
                    for t in range(TC):
                        for e in range(E):
                            last = nc.gpsimd.tensor_scalar(pbt[:, t, e, :], bias2[:, e, :], pr[:, t, e:e + 1], 1.0,
                                                           ALU.mult, ALU.mult)
                    own.link(last)
                    for t in range(TC):
                        last = nc.gpsimd.tensor_tensor(pbs[:, t, :], pbt[:, t, 0, :], pbt[:, t, 1, :], ALU.add)
                    own.link(last)
                    for t in range(TC):
                        last = nc.gpsimd.tensor_tensor(pb[:, t, :], pbs[:, t, :], pbt[:, t, 2, :], ALU.add)
                    last.then_inc(s_pb, 1)
                elif name == "x1":
                    need(pool, s_var, 2 * b + 2)
                    own.step(nc.gpsimd.tensor_tensor(rstd1[:], ve1[:], mhalf[:, 0:TC], ALU.pow))
                    own.wait()
                    pool.sem_inc(s_rstd, 1)

            def residual(b, _):
                need(pool, s_y, b)
                own.link(nc.gpsimd.tensor_tensor(resid[:, 0, :], x1[:, 0, :], bias_o[:], ALU.add))
                nc.gpsimd.tensor_tensor(resid[:, 1, :], x1[:, 1, :], bias_o[:], ALU.add).then_inc(s_res, 1)
                own.end()

            def values(b, _):
                done(pool, b, "vproj", hold=True)
                need(pool, s_o, NG * b, hold=True)
                nc.gpsimd.tensor_copy(vtile[:, :, :, 0:DH], vst[:].rearrange("p c (h d) -> p c h d", h=NH))\
                    .then_inc(s_vt, 1)

            shares = dict(stage=stage, resid=residual, values=values)
            for s in free_again:
                pool.sem_inc(s, CREDIT)
            nc.gpsimd.memset(ident[:], 0.0).then_inc(s_cc, 1)
            pool.wait_ge(s_cc, 1)
            nc.gpsimd.affine_select(out=ident[:], in_=ident[:], compare_op=ALU.not_equal, fill=1.0, base=0,
                                    pattern=[[-1, P]], channel_multiplier=1).then_inc(s_ident, 1)
            nc.gpsimd.memset(ones[:], 1.0)
            nc.gpsimd.memset(onesb[:], 1.0)
            nc.gpsimd.memset(mhalf[:], -0.5)
            nc.gpsimd.memset(vtile[:], 0.0).then_inc(s_cc, 1)
            pool.wait_ge(s_cc, 2)
            pool.wait_ge(s_ident, 1)
            nc.gpsimd.tensor_copy(identb[:], ident[:])
            nc.gpsimd.memset(vtile[:, :, :, DH:DH + 1], 1.0).then_inc(s_const, 1)
            walk(shares, FIRST, None, 0)
            with pool.Fori(0, B - 1) as i:
                walk(shares, ORDER, i, i + 1)
            walk(shares, LAST, B - 1, None)

        @block.scalar
        def _(act):
            def stage(b, name):
                if name == "ctxT":
                    full(act, b, "ctxT")
                    emptied("ctxT", nc.scalar.copy(ctxT[:], bank("ctxT")))
                elif name == "s0":
                    for t in range(TC):
                        need(act, s_nm0, TC * b + t + 1)
                        emptied(f"s0_{t}", nc.scalar.activation(p0[:, t, :], bank(f"s0_{t}"), ACT.Exp,
                                                                bias=nm0[:, t:t + 1], accum_out=sum0[:, t:t + 1]))
                elif name == "p0T":
                    full(act, b, "p0T_0")
                    emptied("p0T_0", nc.scalar.copy(p0T[:, :, 0:P], bank("p0T_0").rearrange("p (c t) -> p c t", c=SC)))
                elif name == "vproj":
                    full(act, b, "vproj")
                    need(act, s_vt, b, hold=True)
                    emptied("vproj", nc.scalar.copy(vst[:].rearrange("p c d -> p (c d)"), bank("vproj")))
                elif name in HIDDEN:
                    k = HIDDEN.index(name)
                    full(act, b, name)
                    for j in range(min(2, NZ - 2 * k)):
                        z = 2 * k + j
                        last = nc.scalar.activation(tz[:, z, :], bank(name)[:, j * T:(j + 1) * T], ACT.Tanh,
                                                    bias=cur[:, V_HALF + z:V_HALF + z + 1], scale=0.5)
                    last.then_inc(s_tz, 1)
                elif name == "lgT":
                    need(act, s_rd, b + 1)
                    nc.scalar.activation(re[:], rd[:], ACT.Exp).then_inc(s_re, 1)
                elif name == "x1":
                    need(act, s_zg, b + 1)
                    nc.scalar.activation(tg[:], zg[:], ACT.Tanh, scale=0.5).then_inc(s_tg, 1)

            def unit(b, u):
                h, half = divmod(u, 2)
                g, j = divmod(h, GH)
                if u % (2 * GH) == 0:
                    need(act, s_o, NG * b + g - 1, hold=True)
                need(act, s_sc, NU * b + u + 1)
                nc.scalar.activation(probs[:, g % 2, j, half * 2 * T:(half + 1) * 2 * T], ps[:, SB + u % 2, :],
                                     ACT.Exp).then_inc(s_pe, 1)

            shares = dict(stage=stage, unit=unit)
            nc.scalar.memzero(k_st[64:P, :, :].rearrange("p h t -> p (h t)").bitcast(F32))
            nc.scalar.memzero(q_st[64:P, :, :].rearrange("p h t -> p (h t)").bitcast(F32)).then_inc(s_zero, 1)
            act.wait_ge(s_pv, PV_COLS)
            nc.scalar.activation(silu_t[:], cols[:, R_COND:R_COND + B], ACT.Tanh, scale=0.5).then_inc(s_ps, 1)
            walk(shares, FIRST, None, 0)
            with act.Fori(0, B - 1) as i:
                walk(shares, ORDER, i, i + 1)
            walk(shares, LAST, B - 1, None)

        @block.tensor
        def _(pe):
            def mm(out, lhsT, rhs, start=True, stop=True):
                return nc.tensor.matmul(out, lhsT, rhs, start=start, stop=stop)

            def turn(out, in_, idn):
                return nc.tensor.transpose(out, in_, idn)

            def prepare():
                step = lambda ins: ins.then_inc(s_pp, 1)
                pe.wait_ge(s_ident, 1)
                pe.wait_ge(s_rows, 16 * 10)
                turn(ps[:, 0, 0:NR], vec_rows[:], ident[0:NR, 0:NR])
                pe.wait_ge(s_wqkv, 16 * 3)
                for i in range(3):
                    last = turn(ps[:, 0, (i + 1) * P:(i + 2) * P], w_qkv[:, i, :], ident[:])
                step(last)
                pe.wait_ge(s_pv, PV_COLS)
                step(mm(ps[:, 1, 0:P], w_qkvT[:, 0, :], w_qkvT[:, 1, :]))
                pe.wait_ge(s_wall, 16 * 17)
                wv_t = w_qkvT[:, 2, :]
                w1f = w1[:, 1, :, :].rearrange("p e r -> p (e r)")
                mm(ps[:, 2, :], wv_t, w1f[:, 0:512])
                mm(ps[:, 3, 0:256], wv_t, w1f[:, 512:768])
                mm(ps[:, 3, 256:256 + P], wv_t, gw1[:, 1, :])
                step(mm(ps[:, 3, 384:384 + E], wv_t, rw[:, 1, :]))
                for k in range(4):
                    turn(ps[:, 4, k * P:(k + 1) * P], w2[:, k, :], ident[:])
                for k in range(2):
                    last = turn(ps[:, 5, k * P:(k + 1) * P], w2[:, 4 + k, :], ident[:])
                step(last)
                cond = cols[:, R_COND:R_COND + B]
                for z in range(NZ):
                    lhsT = gw1[:, 2, :] if z == NZ - 1 else w1[:, 2, z // RC, z % RC * P:(z % RC + 1) * P]
                    mm(ps[:, 6, z * B:(z + 1) * B], lhsT, cond)
                mm(ps[0:E, 6, 32:32 + B], rw[:, 2, :], cond)
                pe.wait_ge(s_pv, PV_SILU)
                for k, w in enumerate((wssq, wssk)):
                    for j in range(2):
                        last = mm(ps[:, 6, 64 + (2 * k + j) * B:64 + (2 * k + j + 1) * B], w[:, j * P:(j + 1) * P],
                                  silu_c[:])
                step(last)
                pe.wait_ge(s_pv, PV_SPREAD)
                for e in range(E):
                    mm(ps[:, 7, e * P:(e + 1) * P], spread[:, e, :], ow[:], stop=False)
                    mm(ps[:, 7, e * P:(e + 1) * P], ones[0:1, :], vec_row[:, 0, :], start=False)
                mm(ps[:, 7, E * P:], spread[:, E, :], wp1[:], stop=False)
                step(mm(ps[:, 7, E * P:], ones[0:1, :], vec_row[:, 1, :], start=False))
                pe.wait_ge(s_pv, PV_W2T)
                for k in range(E * RC):
                    last = mm(ps[:, k // 4, k % 4 * P:(k % 4 + 1) * P], w2T[:, k, :], ow[:])
                step(last)

            def stage(b, stage_name):
                def begin(name):
                    room(pe, b, name)
                    return bank(name)

                if stage_name == "ctxT":
                    o = begin("ctxT")
                    need(pe, s_c, 16 * (b + 1))
                    for c in range(SC):
                        last = turn(o[:, c * P:(c + 1) * P], c_sb[:, c, :], ident[:])
                    filled("ctxT", last)
                elif stage_name == "nxT":
                    o = begin("nxT")
                    need(pe, s_xn, b + 1)
                    for t in range(TC):
                        last = turn(o[:, t * P:(t + 1) * P], xn[:, t, :], ident[:])
                    filled("nxT", last)
                elif stage_name == "qm":
                    o = begin("qm")
                    done(pe, b, "nxT")
                    filled("qm", mm(o[:, 0:T], m_qk[:], nxT[:]))
                elif stage_name == "s0":
                    done(pe, b, "ctxT")
                    done(pe, b, "qm")
                    for t in range(TC):
                        o = begin(f"s0_{t}")
                        filled(f"s0_{t}", mm(o, qmT[:, t * P:(t + 1) * P], ctxT[:]))
                elif stage_name == "hkvT":
                    o = begin("hkvT")
                    need(pe, s_cn, b + 1)
                    for c in range(SC):
                        last = turn(o[:, c * P:(c + 1) * P], cn[:, c, :], ident[:])
                    filled("hkvT", last)
                elif stage_name == "kproj":
                    o = begin("kproj")
                    done(pe, b, "hkvT")
                    filled("kproj", mm(o, wkv1[:, 0:P], xkvT[:]))
                elif stage_name == "p0T":
                    for t in range(TC):
                        o = begin(f"p0T_{t}")
                        need(pe, s_p0, TC * b + t + 1)
                        for c in range(SC):
                            last = turn(o[:, c * P:(c + 1) * P], p0[:, t, c * P:(c + 1) * P], ident[:])
                        filled(f"p0T_{t}", last)
                elif stage_name == "vproj":
                    o = begin("vproj")
                    for c in range(SC):
                        last = mm(o[:, c * P:(c + 1) * P], xkvT[:, c * P:(c + 1) * P], wkv1[:, P:2 * P])
                    filled("vproj", last)
                elif stage_name == "pc":
                    o = begin("pc")
                    done(pe, b, "p0T_0")
                    done(pe, b, "p0T_1")
                    for c in range(SC):
                        last = mm(o[:, 0:T], c_sb[:, c, :], p0T[:, c, :], start=(c == 0), stop=(c == SC - 1))
                    filled("pc", last)
                elif stage_name in HIDDEN:
                    k = HIDDEN.index(stage_name)
                    o = begin(stage_name)
                    if k == 0:
                        done(pe, b, "pc")
                    for j in range(2):
                        z = 2 * k + j
                        if z < NZ - 1:
                            wa, wb = w1[:, 0, z // RC, z % RC * P:(z % RC + 1) * P], w1ev[:, z * P:(z + 1) * P]
                            oz = o[:, j * T:(j + 1) * T]
                        elif z == NZ - 1:
                            wa, wb, oz = gw1[:, 0, :], gw1ev[:], o[:, 0:T]
                        else:
                            wa, wb, oz = rw[:, 0, :], rwev[:], o[0:E, T:2 * T]
                        mm(oz, wa, nxT[:], stop=False)
                        last = mm(oz, wb, pcT[:], start=False)
                    filled(stage_name, last)
                elif stage_name == "lgT":
                    o = begin("lgT")
                    done(pe, b, "hid_3")
                    pe.sem_inc(s_tick, 1)
                    for t in range(TC):
                        last = turn(o[:, t * E:(t + 1) * E], lg[:, t * P:(t + 1) * P], ident[0:E, 0:E])
                    filled("lgT", last)
                elif stage_name == "eo":
                    for t in range(TC):
                        o = begin(f"eo_{t}")
                        for e in range(E):
                            for k in range(RC):
                                mm(o[:, e * P:(e + 1) * P], hT[:, e * RC + k, t * P:(t + 1) * P],
                                   w2o[:, e * RC + k, :], start=(k == 0), stop=(k == RC - 1))
                        filled(f"eo_{t}", mm(o[:, E * P:], hT[:, NZ - 1, t * P:(t + 1) * P], gw2[:]))
                elif stage_name == "xqT":
                    o = begin("xqT")
                    need(pe, s_xn1, b + 1)
                    for t in range(TC):
                        last = turn(o[:, t * P:(t + 1) * P], xn1[:, t, :], ident[:])
                    filled("xqT", last)
                elif stage_name == "qproj":
                    o = begin("qproj")
                    done(pe, b, "xqT")
                    filled("qproj", mm(o[:, 0:T], wq1[:], xqT[:]))

            def maxima_bank(b, m):
                need(pe, s_xd[m % 2], b * MHALF + m // 2, hold=True)
                return ps[:, XB + m % 2, :]

            def tile(b, gk):
                g, k = gk
                h, t = g * GH + k // TC, k % TC
                m = MAXIMA.index(("tile", gk))
                if k == 0:
                    need(pe, s_st[g // 2], (b + 1) * ST_DMAS * 16)
                    pe.sem_inc(s_tick, 1)
                o = maxima_bank(b, m)
                mm(o, q_st[0:KR, h, t * P:(t + 1) * P], k_st[0:KR, h, :]).then_inc(s_xf[m % 2], 1)

            def rows(b, g):
                m = MAXIMA.index(("rows", g))
                need(pe, s_mp, NG * b + g + 1, hold=True)
                o = maxima_bank(b, m)[0:NP * GH, :].bitcast(BF16)
                for t in range(TC):
                    last = turn(o[:, t * P:(t + 1) * P],
                                mparts[:, t, :, :].rearrange("p i h -> p (i h)"), identb[:])
                last.then_inc(s_xf[m % 2], 1)

            def unit(b, u):
                h, half = divmod(u, 2)
                g = h // GH
                if u % (2 * GH) == 0:
                    need(pe, s_mrow[g % 2], 16 * (2 * b + g // 2 + 1), hold=True)
                need(pe, s_pe, NU * b + u - 1)
                for j in range(2):
                    c = 2 * half + j
                    last = mm(ps[:, SB + u % 2, j * T:(j + 1) * T], k_st[:, h, c * P:(c + 1) * P], q_st[:, h, :])
                last.then_inc(s_sc, 1)

            def pv(b, g):
                if g == 0:
                    need(pe, s_vt, b + 1)
                need(pe, s_pe, NU * b + 2 * (g + 1) * GH)
                need(pe, s_od[g % 2], 4 * b + g // 2)
                for c in range(SC):
                    for j in range(GH):
                        last = mm(ps[j * QT:(j + 1) * QT, OB + g % 2, 0:T], vtile[:, c, g * GH + j, :],
                                  probs[:, g % 2, j, c * T:(c + 1) * T], start=(c == 0), stop=(c == SC - 1))
                last.then_inc(s_o, 1)

            def after(b, n):
                if n < 2:
                    t = n
                    need(pe, s_od[t], 4 * b + 2)
                    if t == 0:
                        need(pe, s_od[1], 4 * b + 2)
                    for g in range(NG):
                        last = turn(ps[:, OB + t, g * P:(g + 1) * P], o_sb[:, g, t * P:(t + 1) * P], ident[:])
                elif n == 2:
                    for t in range(TC):
                        need(pe, s_od[t], 4 * b + 3)
                    for t in range(TC):
                        last = turn(ps[:, OB, t * P:(t + 1) * P], on[:, t, :], ident[:])
                else:
                    need(pe, s_od[0], 4 * b + 4)
                    for t in range(TC):
                        last = mm(ps[:, OB + 1, t * P:(t + 1) * P], onT[:, t * P:(t + 1) * P], wp1[:])
                last.then_inc(s_post, 1)

            shares = dict(stage=stage, tile=tile, rows=rows, unit=unit, pv=pv, after=after)
            prepare()
            pe.wait_ge(s_pv, PV_ALL)
            pe.wait_ge(s_ones, 16)
            walk(shares, FIRST, None, 0)
            with pe.Fori(0, B - 1) as i:
                walk(shares, ORDER, i, i + 1)
            walk(shares, LAST, B - 1, None)

        @block.vector
        def _(dve):
            V = nc.vector

            def prepare():
                prep = Chain(dve, s_pv, PV_ALL)
                prep.begin(0)
                dve.wait_ge(s_pp, 1)
                V.tensor_copy(cols[:], ps[:, 0, 0:NR])
                prep.step(V.tensor_copy(w_qkvT[:].rearrange("p a n -> p (a n)"), ps[:, 0, P:]))
                assert prep.n == PV_COLS
                dve.wait_ge(s_pp, 2)
                V.tensor_scalar(m_qk[:], ps[:, 1, 0:P], SCALE0, None, ALU.mult)
                dve.wait_ge(s_ps, 1)
                prep.wait()
                prep.link(V.scalar_tensor_tensor(silu_c[:], silu_t[:], 1.0, cols[:, R_COND:R_COND + B],
                                                 ALU.add, ALU.mult))
                prep.step(V.tensor_scalar(silu_c[:], silu_c[:], 0.5, None, ALU.mult))
                assert prep.n == PV_SILU
                dve.wait_ge(s_const, 1)
                for e in range(E):
                    V.tensor_scalar(spread[:, e, :], ones[:], cols[:, R_EB2 + e:R_EB2 + e + 1], None, ALU.mult)
                prep.step(V.tensor_scalar(spread[:, E, :], ones[:], cols[:, R_BV:R_BV + 1], None, ALU.mult))
                dve.wait_ge(s_pp, 3)
                V.tensor_copy(w1ev[:, 0:512], ps[:, 2, :])
                V.tensor_copy(w1ev[:, 512:768], ps[:, 3, 0:256])
                V.tensor_copy(gw1ev[:], ps[:, 3, 256:384])
                V.tensor_copy(rwev[:], ps[:, 3, 384:384 + E])
                dve.wait_ge(s_pp, 4)
                V.tensor_copy(w2T[:, 0:4, :].rearrange("p a n -> p (a n)"), ps[:, 4, :])
                prep.step(V.tensor_copy(w2T[:, 4:6, :].rearrange("p a n -> p (a n)"), ps[:, 5, 0:256]))
                assert prep.n == PV_W2T
                dve.wait_ge(s_pp, 5)
                V.tensor_tensor(allv[:, :, V_Z:V_Z + NZ].rearrange("p b z -> p z b"),
                                ps[:, 6, 0:NZ * B].rearrange("p (z b) -> p z b", b=B),
                                cols[:, R_B1:R_B1 + NZ].unsqueeze(2).to_broadcast([P, NZ, B]), ALU.add)
                V.tensor_tensor(allv[:, :, V_ADA:V_ADA + 4].rearrange("p b z -> p z b"),
                                ps[:, 6, 64:64 + 4 * B].rearrange("p (z b) -> p z b", b=B),
                                cols[:, R_SSQ:R_SSQ + 4].unsqueeze(2).to_broadcast([P, 4, B]), ALU.add)
                prep.link(V.tensor_scalar(rball[:], ps[0:E, 6, 32:32 + B], rb[:, 0:1], None, ALU.add))
                V.tensor_scalar(allv[:, :, V_HALF:V_HALF + NZ], allv[:, :, V_Z:V_Z + NZ], 0.5, None, ALU.mult)
                for k in range(2):
                    z = V_ADA + 2 * k
                    prep.step(V.tensor_scalar(allv[:, :, z:z + 1], allv[:, :, z:z + 1], 1.0, None, ALU.add))
                dve.wait_ge(s_pp, 6)
                V.tensor_copy(bias2[:].rearrange("p a n -> p (a n)"), ps[:, 7, 0:E * P])
                V.tensor_copy(bias_o[:], ps[:, 7, E * P:])
                dve.wait_ge(s_pp, 7)
                V.tensor_copy(w2o[:, 0:4, :].rearrange("p a n -> p (a n)"), ps[:, 0, :])
                prep.link(V.tensor_copy(w2o[:, 4:6, :].rearrange("p a n -> p (a n)"), ps[:, 1, 0:256]))
                prep.end()

            own = Chain(dve, s_cv, 22)
            late = Chain(dve, s_cm, 2)
            top = Chain(dve, s_cx, 4)

            def stage(b, stage_name):
                if stage_name == "start":
                    own.begin(b)
                    need(dve, s_x, 16 * (b + 1))
                    for t in range(TC):
                        V.bn_stats(stats[:, t, :], x_sb[:, t, :])
                    need(dve, s_c, 16 * (b + 1))
                    for c in range(SC):
                        last = V.bn_stats(stats[:, TC + c, :], c_sb[:, c, :])
                    own.link(last)
                    at_b = slice(b, b + 1) if isinstance(b, int) else bass.ds(b, 1)
                    V.tensor_copy(rcur[:], rball[:, at_b])
                    for t in range(TC + SC):
                        last = V.bn_aggr(mv[:, t, :], stats[:, t, :])
                    V.tensor_copy(cur[:], allv[:, at_b, :].rearrange("p a v -> p (a v)"))
                    own.link(last)
                    V.tensor_scalar(ve[:], mv[:, :, 1], EPS, None, ALU.add).then_inc(s_var, 1)
                elif stage_name == "nxT":
                    need(dve, s_rstd, 2 * b + 1)
                    for t in range(TC):
                        last = V.tensor_scalar(xn[:, t, :], x_sb[:, t, :], mv[:, t, 0:1], rstd[:, t:t + 1],
                                               ALU.subtract, ALU.mult)
                    last.then_inc(s_xn, 1)
                    for c in range(SC):
                        last = V.tensor_scalar(cn[:, c, :], c_sb[:, c, :], mv[:, TC + c, 0:1],
                                               rstd[:, TC + c:TC + c + 1], ALU.subtract, ALU.mult)
                    last.then_inc(s_cn, 1)
                    full(dve, b, "nxT")
                    emptied("nxT", V.tensor_scalar(nxT[:], bank("nxT")[:, 0:T], cols[:, R_GAMMA:R_GAMMA + 1],
                                                   cols[:, R_BETA:R_BETA + 1], ALU.mult, ALU.add))
                elif stage_name == "qm":
                    full(dve, b, "qm")
                    emptied("qm", V.tensor_copy(qmT[:], bank("qm")[:, 0:T]))
                elif stage_name == "s0":
                    for t in range(TC):
                        full(dve, b, f"s0_{t}")
                        V.tensor_reduce(nm0[:, t:t + 1], bank(f"s0_{t}"), AX_X, ALU.max, negate=True)\
                            .then_inc(s_nm0, 1)
                elif stage_name == "hkvT":
                    full(dve, b, "hkvT")
                    emptied("hkvT", V.tensor_scalar(xkvT[:], bank("hkvT"), cur[:, V_ADA + 2:V_ADA + 3],
                                                    cur[:, V_ADA + 3:V_ADA + 4], ALU.mult, ALU.add))
                    for t in range(TC):
                        done(dve, b, f"s0_{t}")
                        own.link(V.reciprocal(rs0[:, t:t + 1], sum0[:, t:t + 1]))
                        V.tensor_scalar(p0[:, t, :], p0[:, t, :], rs0[:, t:t + 1], None, ALU.mult)\
                            .then_inc(s_p0, 1)
                elif stage_name == "kproj":
                    full(dve, b, "kproj")
                    need(dve, s_kp, b)
                    emptied("kproj", V.tensor_scalar(kf[:], bank("kproj"), cols[:, R_BK:R_BK + 1], None, ALU.add))
                elif stage_name == "p0T":
                    full(dve, b, "p0T_1")
                    emptied("p0T_1", V.tensor_copy(p0T[:, :, P:T],
                                                   bank("p0T_1").rearrange("p (c t) -> p c t", c=SC)))
                elif stage_name == "pc":
                    full(dve, b, "pc")
                    emptied("pc", V.tensor_copy(pcT[:], bank("pc")[:, 0:T]))
                elif stage_name in ACTIVATED:
                    k = ACTIVATED.index(stage_name)
                    name = HIDDEN[k]
                    need(dve, s_sg, 4 * b + k + 1)
                    for j in range(min(2, NZ - 2 * k)):
                        z = 2 * k + j
                        last = V.scalar_tensor_tensor(hT[:, z, :], bank(name)[:, j * T:(j + 1) * T],
                                                      cur[:, V_Z + z:V_Z + z + 1], tz[:, z, :], ALU.add, ALU.mult)
                    if k == 3:
                        last = V.tensor_scalar(lg[:], bank(name)[0:E, T:2 * T], rcur[:, 0:1], None, ALU.add)
                    emptied(name, last)
                elif stage_name == "lgT":
                    full(dve, b, "lgT")
                    lgT = bank("lgT")[:, 0:TC * E].rearrange("p (t e) -> p t e", e=E)
                    own.link(V.tensor_reduce(rmx[:], lgT, AX_X, ALU.max))
                    own.step(V.tensor_tensor(rd[:], lgT, rmx[:].unsqueeze(2).to_broadcast([P, TC, E]),
                                             ALU.subtract))
                    own.wait()
                    dve.sem_inc(s_rd, 1)
                    need(dve, s_re, b + 1)
                    own.link(V.tensor_reduce(rsum[:], re[:], AX_X, ALU.add))
                    own.link(V.reciprocal(rinv[:], rsum[:]))
                    emptied("lgT", V.tensor_tensor(pr[:], re[:], rinv[:].unsqueeze(2).to_broadcast([P, TC, E]),
                                                   ALU.mult))
                    done(dve, b, "lgT")
                    dve.sem_inc(s_pr, 1)
                elif stage_name == "eo":
                    need(dve, s_pb, b + 1)
                    for t in range(TC):
                        name = f"eo_{t}"
                        o = bank(name)
                        full(dve, b, name)
                        for e in range(E):
                            prev = pb[:, t, :] if e == 0 else yacc[:, e - 1, t, :]
                            own.link(V.scalar_tensor_tensor(yacc[:, e, t, :], o[:, e * P:(e + 1) * P],
                                                            pr[:, t, e:e + 1], prev, ALU.mult, ALU.add))
                        emptied(name, V.tensor_tensor(zg[:, t, :], o[:, E * P:], bias_g[:], ALU.add))
                    for t in range(TC):
                        done(dve, b, f"eo_{t}")
                    dve.sem_inc(s_zg, 1)
                elif stage_name == "x1":
                    need(dve, s_tg, b + 1)
                    own.link(V.scalar_tensor_tensor(ug[:], tg[:], 1.0, yacc[:, E - 1, :, :], ALU.add, ALU.mult))
                    need(dve, s_res, b)
                    own.link(V.scalar_tensor_tensor(x1[:], ug[:], 0.5, x_sb[:], ALU.mult, ALU.add))
                    dve.sem_inc(s_x1, 1)
                    for t in range(TC):
                        last = V.bn_stats(st1[:, t, :], x1[:, t, :])
                    own.link(last)
                    V.tensor_copy(rmx[:], rinv[:])
                    for t in range(TC):
                        last = V.bn_aggr(mv1[:, t, :], st1[:, t, :])
                    own.link(last)
                    V.tensor_scalar(ve1[:], mv1[:, :, 1], EPS, None, ALU.add).then_inc(s_var, 1)
                elif stage_name == "xqT":
                    need(dve, s_rstd, 2 * b + 2)
                    for t in range(TC):
                        last = V.tensor_scalar(xn1[:, t, :], x1[:, t, :], mv1[:, t, 0:1], rstd1[:, t:t + 1],
                                               ALU.subtract, ALU.mult)
                    last.then_inc(s_xn1, 1)
                    full(dve, b, "xqT")
                    emptied("xqT", V.tensor_scalar(xqT[:], bank("xqT")[:, 0:T], cur[:, V_ADA:V_ADA + 1],
                                                   cur[:, V_ADA + 1:V_ADA + 2], ALU.mult, ALU.add))
                elif stage_name == "qproj":
                    full(dve, b, "qproj")
                    emptied("qproj", V.tensor_scalar(qf[:], bank("qproj")[:, 0:T], cols[:, R_BQ:R_BQ + 1], SCALE1,
                                                     ALU.add, ALU.mult))
                    done(dve, b, "qproj")
                    need(dve, s_qscr, b * NP * 16)
                    own.link(V.tensor_copy(qp[:, 0, :], qf[:]))
                    own.link(V.tensor_tensor(qr[:, 0, :], qf[:], qp[:, 0, :], ALU.subtract))
                    own.link(V.tensor_copy(qp[:, 1, :], qr[:, 0, :]))
                    own.link(V.tensor_tensor(qr[:, 1, :], qr[:, 0, :], qp[:, 1, :], ALU.subtract))
                    V.tensor_copy(qp[:, 2, :], qr[:, 1, :]).then_inc(s_qp, 1)
                    own.end()

            def tile(b, gk):
                g, k = gk
                h, t = g * GH + k // TC, k % TC
                m = MAXIMA.index(("tile", gk))
                need(dve, s_xf[m % 2], b * MHALF + m // 2 + 1)
                V.tensor_reduce(mx[:, t, h:h + 1], ps[:, XB + m % 2, :], AX_X, ALU.max, negate=True)\
                    .then_inc(s_xd[m % 2], 1)
                if k == GH * TC - 1:
                    top.begin(NG * b + g)
                    for turn_of in (m, m - 1):
                        need(dve, s_xd[turn_of % 2], b * MHALF + turn_of // 2 + 1)
                    mg = mx[:, :, g * GH:(g + 1) * GH]
                    top.link(V.tensor_copy(mparts[:, :, 0, :], mg))
                    top.link(V.tensor_tensor(mr[:, 0], mg, mparts[:, :, 0, :], ALU.subtract))
                    top.link(V.tensor_copy(mparts[:, :, 1, :], mr[:, 0]))
                    top.link(V.tensor_tensor(mr[:, 1], mr[:, 0], mparts[:, :, 1, :], ALU.subtract))
                    V.tensor_copy(mparts[:, :, 2, :], mr[:, 1]).then_inc(s_mp, 1)
                    top.end()

            def rows(b, g):
                m = MAXIMA.index(("rows", g))
                need(dve, s_mrow[g % 2], 16 * (2 * b + g // 2))
                need(dve, s_xf[m % 2], b * MHALF + m // 2 + 1)
                V.tensor_copy(mT[:, g % 2, :], ps[0:NP * GH, XB + m % 2, :].bitcast(BF16)[:, 0:T])\
                    .then_inc(s_xd[m % 2], 1)

            def pv(b, g):
                need(dve, s_o, NG * b + g + 1)
                V.tensor_copy(o_sb[:, g, :], ps[:, OB + g % 2, 0:T]).then_inc(s_od[g % 2], 1)

            def after(b, n):
                if n < 2:
                    t = n
                    if t == 0:
                        late.begin(b)
                    o = ps[:, OB + t, :].rearrange("p (h q) -> p h q", q=QT)
                    need(dve, s_post, 4 * b + t + 1)
                    late.link(V.reciprocal(rs1[:, t, :], o[:, :, DH]))
                    V.tensor_tensor(on[:, t, :].rearrange("p (h d) -> p h d", d=DH), o[:, :, 0:DH],
                                    rs1[:, t, :].unsqueeze(2).to_broadcast([P, NH, DH]), ALU.mult)\
                        .then_inc(s_od[t], 1)
                elif n == 2:
                    need(dve, s_post, 4 * b + 3)
                    V.tensor_copy(onT[:], ps[:, OB, 0:T]).then_inc(s_od[0], 1)
                else:
                    need(dve, s_post, 4 * b + 4)
                    need(dve, s_res, b + 1)
                    need(dve, s_out, 16 * b)
                    V.tensor_tensor(y_sb[:], ps[:, OB + 1, 0:T].rearrange("p (t d) -> p t d", d=P), resid[:],
                                    ALU.add).then_inc(s_od[1], 1)
                    need(dve, s_od[1], 4 * b + 4)
                    dve.sem_inc(s_y, 1)
                    late.end()

            shares = dict(stage=stage, tile=tile, rows=rows, pv=pv, after=after)
            prepare()
            walk(shares, FIRST, None, 0)
            with dve.Fori(0, B - 1) as i:
                walk(shares, ORDER, i, i + 1)
            walk(shares, LAST, B - 1, None)


_INS = [
    "x", "cond_1024", "ctx_1024", "L0_xcond_ln_gamma", "L0_xcond_ln_beta", "L0_xcond_Wq", "L0_xcond_Wk",
    "L0_xcond_Wv", "L0_xcond_router_W", "L0_xcond_router_b", "L0_xcond_e_w1", "L0_xcond_e_b1", "L0_xcond_e_w2",
    "L0_xcond_e_b2", "L0_xcond_gate_w1", "L0_xcond_gate_b1", "L0_xcond_gate_w2", "L0_xcond_gate_b2",
    "L0_xcond_out_w", "L0_xcond_out_b", "L1_xcond_Wq", "L1_xcond_bq", "L1_xcond_Wkv", "L1_xcond_bkv",
    "L1_xcond_Wp", "L1_xcond_bp", "L1_xcond_Wss_q", "L1_xcond_bss_q", "L1_xcond_Wss_kv", "L1_xcond_bss_kv",
]


def kernel(**inputs):
    import numpy as _np
    import concourse.bacc as _bacc
    from concourse import mybir as _mybir
    from concourse.bass_utils import run_bass_kernel_spmd as _run

    nc = _bacc.Bacc("TRN2", target_bir_lowering=False, num_devices=1)
    arrays, aps = {}, {}
    for name in _INS:
        array = _np.ascontiguousarray(inputs[name])
        arrays[f"in_{name}"] = array
        aps[name] = nc.dram_tensor(f"in_{name}", array.shape, _mybir.dt.from_np(array.dtype),
                                   kind="ExternalInput").ap()
    out = nc.dram_tensor("out_0", (B, T, P), _mybir.dt.float32, kind="ExternalOutput").ap()
    build(nc, aps, out)
    r = _run(nc, [arrays], core_ids=[0])
    return r.results[0]["out_0"]
```

```python
from contextlib import ExitStack

import concourse.bass as bass
from concourse import mybir

F32 = mybir.dt.float32
BF16 = mybir.dt.bfloat16
ACT = mybir.ActivationFunctionType
ALU = mybir.AluOpType
AX_X = mybir.AxisListType.X

P = 128
B = 4
T, TC = 256, 2
S, SC = 512, 4
E, RC = 3, 2
NH, DH = 16, 8
GH = 4
NG = NH // GH
PV_EARLY, PV_SILU, PV_WV, PV_W2T, PV_PARTS, PV_ROWS, PV_ALL = 1, 2, 3, 4, 10, 11, 12
QT = 32
NZ = E * RC + 1
NP = 3
KR = NP * NP * DH
EPS = 1e-5
SCALE0 = float(P) ** -0.5
SCALE1 = float(DH) ** -0.5

R_B1, R_GB1, R_BQ, R_BK, R_BV, R_SSQ, R_SSK = 0, 6, 7, 8, 9, 10, 12
R_COND, R_EB2, R_OB, R_GB2, R_BP = 14, 18, 21, 22, 23
NR = 24
R_GAMMA, R_BETA = 0, 1
NBZ = NZ + 1
C_EB = B * NBZ
C_GB = C_EB + E
C_BO = C_GB + 1
NCB = C_BO + 1
NADA = 4

FRONT = ["ctxT", "nxT", "qm", "s0_0", "s0_1", "p0T_0", "p0T_1", "pc"]
BACK = ["hkvT", "lgT", "hid_0", "hid_1", "kproj", "vproj", "hid_2", "hid_3", "eo_0", "eo_1", "xqT", "qproj"]
MHALF = NG * (GH * TC + 1) // 2
NU = 2 * NH

FRONT_STAGES = ["start", "ctxT", "xn", "nxT", "qm", "s0_0", "s0_1", "p0_0", "p0T_0", "p0_1", "p0T_1", "pc"]
BACK_STAGES = ["hkvT", "lgT", "hid_0", "hid_1", "act_0", "kproj", "act_1", "vproj", "route", "hid_2", "hid_3",
               "act_2", "act_3", "eo_0", "eo_1", "x1", "xn1", "xqT", "qproj", "q_parts"]
BY_SCALARE = ["ctxT", "hkvT", "kproj", "nxT", "p0T_0", "p0T_1", "pc", "qm", "vproj"]


def maxima_steps():
    steps = []
    for g in range(NG + 1):
        for k in range(GH * TC):
            if g < NG:
                steps.append(("tile", (g, k)))
            if g > 0:
                steps += [("part", (g - 1, k))] if k < 2 * NP - 1 else [("rows", g - 1)] if k == 2 * NP - 1 else []
    return steps


MAXIMA = [step for step in maxima_steps() if step[0] != "part"]


def placed(start, end, steps):
    return [(start + (n + 0.5) / len(steps) * (end - start), step) for n, step in enumerate(steps)]


def schedule(engine, plan):
    steps, at = [], {}

    def place(when, step):
        at[step] = when
        steps.append((when, step))

    groups = plan["maxima"]
    for n, step in enumerate(maxima_steps()):
        if n < EARLY:
            continue
        if step[0] == "tile":
            g, k = step[1]
            when = groups[g] + (k + 0.5) / (GH * TC) * (groups[g + 1] - groups[g])
        elif n >= len(maxima_steps()) - 2 * NP:
            when += 0.004
        place(when + n * 1e-7, ("this", *step))
    starts, before = plan["heads"], 0.0
    for u in range(NU):
        g, j = divmod(u, 2 * GH)
        if j == 0:
            first = max(starts[g], before, at.get(("this", "rows", g), 0.0) + 0.01)
        before = first + (j + 0.5) * (starts[g + 1] - starts[g]) / (2 * GH)
        place(before, ("this", "unit", u))
        if j == PV_LAG and g > 0:
            place(before + 1e-5, ("this", "pv", g - 1))
    place(before + 1e-5, ("this", "pv", NG - 1))
    for when, name in placed(*plan["back"], BACK_STAGES):
        place(when, ("next", "stage", name))
    turned, hidden = at["next", "stage", "hkvT"], at["next", "stage", "hid_3"]
    for when, name in placed(*plan["context"], FRONT_STAGES[:3]):
        place(max(when, turned + 1e-3) + 1e-6 * FRONT_STAGES.index(name), ("ahead", "stage", name))
    last = max(hidden, at["ahead", "stage", "xn"])
    for when, name in placed(*plan["evidence"], FRONT_STAGES[3:]):
        last = max(when, last + 1e-4)
        place(last, ("ahead", "stage", name))
    for when, n in placed(max(plan["after"][0], before + 2e-5), max(plan["after"][1], before + 3e-5), range(4)):
        place(when, ("this", "after", n))
    place(-1.0, ("ahead", "load", 0))
    for n in range(2 * NP - 1):
        place(at["next", "stage", "kproj"] + (n + 0.5) * plan["k_split"], ("next", "k_part", n))
    k_out = max(at["next", "stage", "kproj"] + plan["k_out"], at["next", "k_part", 2 * NP - 2] + 1e-5)
    q_out = at["next", "stage", "q_parts"]
    half, all_heads = at["this", "unit", NU // 2 - 1] + plan["k_in"], at["this", "unit", NU - 1]
    place(k_out, ("next", "k_out", 0))
    place(max(k_out, half) + 1e-5, ("next", "k_in", 0))
    place(q_out, ("next", "q_out", 0))
    place(q_out + 1e-5, ("ahead", "load_x", 0))
    place(max(k_out, half, q_out) + 2e-5, ("next", "q_in", 0))
    place(max(k_out, half, all_heads) + 3e-5, ("next", "k_in", 1))
    place(max(k_out, half, all_heads, q_out) + 4e-5, ("next", "q_in", 1))
    begin = max(plan["early"][0], q_out + 1e-3)
    for when, step in placed(begin, max(plan["early"][1], begin + 0.02), maxima_steps()[:EARLY]):
        place(when, ("next", *step))
    later = LATER.get(engine, {})
    order = []
    for n, (when, (whose, kind, which)) in enumerate(steps):
        share = "maxima" if kind in ("tile", "part", "rows") else f"{whose} {kind}"
        order.append((when + later.get(share, 0.0), n, (whose, kind, which)))
    order.sort(key=lambda placed_step: placed_step[:2])
    return [("this", "values", 0)] + [step for _, _, step in order] + [("next", "resid", 0), ("this", "store", 0)]


LATER = {
    "act": {"this unit": 0.0, "next stage": 0.0, "ahead stage": 0.013},
    "dve": {"this pv": -0.0, "next stage": 0.0, "ahead stage": -0.007, "this after": -0.005, "maxima": -0.013},
    "sp": {"maxima": -0.08}
}
PV_LAG = 4
EARLY = 8
PLAN = {
    "maxima": (0.0, 0.01, 0.15, 0.3, 0.432), "heads": (0.147, 0.322, 0.509, 0.69, 0.866), "back": (0.0, 0.72),
    "context": (0.3, 0.385), "evidence": (0.413, 1.018), "after": (0.88, 0.955), "k_out": 0.26, "k_in": 0.253,
    "early": (0.86, 1.0), "k_split": 0.002
}
FIRST_PLAN = {
    "maxima": (0, 0.079, 0.178, 0.4, 0.56), "heads": (0.264, 0.425, 0.586, 0.813, 0.885), "back": (0.0, 0.75),
    "context": (0.534, 0.632), "evidence": (0.66, 1.008), "after": (0.9, 1.0), "k_out": 0.072, "k_in": 0.043,
    "early": (0.98, 1.1), "k_split": 0.03
}
LAST_PLAN = {
    "maxima": (0.0, 0.01, 0.152, 0.315, 0.462), "heads": (0.213, 0.378, 0.542, 0.707, 0.872), "back": (0.17, 0.689),
    "context": (0.305, 0.403), "evidence": (0.417, 0.927), "after": (1.2, 1.3), "k_out": 0.081, "k_in": 0.081,
    "early": (0.87, 0.972), "k_split": 0.04
}
ENGINES = ("pe", "act", "dve", "pool", "sp")

ORDER = {engine: schedule(engine, PLAN) for engine in ENGINES}
FIRST = [("next", "prep" if isinstance(step, int) else "stage", step)
         for step in ("start", "ctxT", 1, "xn", "nxT", 2, "qm", "s0_0", 4, 3, "s0_1", "p0_0", 5, "p0T_0", "p0_1", 6,
                      "p0T_1", 7, "pc")]
PREP = [which for _, kind, which in FIRST if kind == "prep"] + [8]


def first_period(engine):
    order = [step for step in schedule(engine, FIRST_PLAN) if step[0] != "this"]
    last_prep = order.index(("next", "stage", "act_0"))
    return FIRST + order[:last_prep] + [("next", "prep", 8)] + order[last_prep:]


def last_but_one_period(engine):
    return [step for step in ORDER[engine] if step[0] != "ahead"]


def last_period(engine):
    return [step for step in schedule(engine, LAST_PLAN) if step[0] == "this"]


def walk(shares, order, this, following, ahead):
    for whose, kind, which in order:
        if kind in shares:
            shares[kind]({"this": this, "next": following, "ahead": ahead}[whose], which)


HIDDEN = [f"hid_{k}" for k in range(4)]
ACTIVATED = [f"act_{k}" for k in range(4)]


def turn_of(name):
    if name in FRONT:
        return 2, len(FRONT), FRONT.index(name)
    k = BACK.index(name)
    return k % 2, len(BACK) // 2, k // 2


CREDIT = 32


class Chain:

    def __init__(self, eng, sem, per):
        self.eng, self.sem, self.per = eng, sem, per

    def begin(self, b):
        self.base, self.n = b * self.per, 0

    def step(self, ins):
        self.n += 1
        ins.then_inc(self.sem, 1)

    def link(self, ins):
        self.step(ins)
        self.wait()

    def wait(self):
        self.eng.wait_ge(self.sem, self.base + self.n)

    def end(self):
        assert self.n == self.per, (self.n, self.per)


def build(nc, a, out):
    with ExitStack() as ctx:
        def sb(name, shape, dt=F32):
            return ctx.enter_context(nc.sbuf_tensor(name, shape, dt))

        def sem(name):
            return ctx.enter_context(nc.semaphore(name))

        vec_rows = sb("vec_rows", [NR, P])
        early_rows = sb("early_rows", [2, P])
        early_cols = sb("early_cols", [P, 2])
        cols = sb("cols", [P, NR])
        w_qkv = sb("w_qkv", [P, 3, P])
        w_qkvT = sb("w_qkvT", [P, 3, P])
        w1 = sb("w1", [P, 3, E, RC * P])
        gw1 = sb("gw1", [P, 3, P])
        rw = sb("rw", [P, 3, E])
        rb = sb("rb", [E, 1])
        w2 = sb("w2", [P, E * RC, P])
        w2T = sb("w2T", [P, E * RC, P])
        gw2 = sb("gw2", [P, P])
        ow = sb("ow", [P, P])
        wq1 = sb("wq1", [P, P])
        wkv1 = sb("wkv1", [P, 2 * P])
        wp1 = sb("wp1", [P, P])
        wssq = sb("wssq", [P, 2 * P])
        wssk = sb("wssk", [P, 2 * P])
        m_qk = sb("m_qk", [P, P])
        w1ev = sb("w1ev", [P, E * RC * P])
        gw1ev = sb("gw1ev", [P, P])
        rwev = sb("rwev", [P, E])
        w2o = sb("w2o", [P, E * RC, P])
        gw2h = sb("gw2h", [P, P])
        silu_t = sb("silu_t", [P, B])
        silu_c = sb("silu_c", [P, B])
        biases = sb("biases", [P, NCB])
        bias_r = sb("bias_r", [P, 2, NCB])
        bias_p = sb("bias_p", [P, NP, NCB], BF16)
        bias_t = sb("bias_t", [NP * NCB, P], BF16)
        bias_rows = sb("bias_rows", [NP, NCB, P], BF16)
        bias_cur = sb("bias_cur", [NP, NBZ, P], BF16)
        ident = sb("ident", [P, P])
        identb = sb("identb", [P, P], BF16)
        onesb = sb("onesb", [NP * NH * S // T, T], BF16)
        ada = sb("ada", [P, B, NADA])
        cur = sb("cur", [P, NADA])
        mhalf = sb("mhalf", [P, TC + SC])

        x_sb = sb("x_sb", [P, TC, P])
        x_again = sb("x_again", [P, TC, P])
        c_sb = sb("c_sb", [P, SC, P])
        stats = sb("stats", [P, TC + SC, 6])
        mv = sb("mv", [P, TC + SC, 2])
        ve = sb("ve", [P, TC + SC])
        rstd = sb("rstd", [P, TC + SC])
        xn = sb("xn", [P, TC, P])
        cn = sb("cn", [P, SC, P])
        ctxT = sb("ctxT", [P, S])
        nxT = sb("nxT", [P, T])
        qmT = sb("qmT", [P, T])
        nm0 = sb("nm0", [P, TC])
        sum0 = sb("sum0", [P, TC])
        rs0 = sb("rs0", [P, TC])
        p0 = sb("p0", [P, TC, S])
        p0T = sb("p0T", [P, SC, T])
        pcT = sb("pcT", [P, T])
        tz = sb("tz", [P, 8, T])
        hT = sb("hT", [P, 8, T])
        rmx = sb("rmx", [P, TC])
        rd = sb("rd", [P, TC, E])
        re = sb("re", [P, TC, E])
        rsum = sb("rsum", [P, TC])
        rinv = sb("rinv", [P, TC])
        pr = sb("pr", [P, TC, E])
        yacc = sb("yacc", [P, 3, TC, P])
        tg = sb("tg", [P, TC, P])
        ug = sb("ug", [P, TC, P])
        x1 = sb("x1", [P, TC, P])
        st1 = sb("st1", [P, TC, 6])
        mv1 = sb("mv1", [P, TC, 2])
        ve1 = sb("ve1", [P, TC])
        rstd1 = sb("rstd1", [P, TC])
        xn1 = sb("xn1", [P, TC, P])
        resid = sb("resid", [P, TC, P])
        xkvT = sb("xkvT", [P, S])
        xqT = sb("xqT", [P, T])
        kf = sb("kf", [P, S])
        kr = sb("kr", [P, 2, S])
        kp = sb("kp", [P, NP, S], BF16)
        qf = sb("qf", [P, T])
        qr = sb("qr", [P, 2, T])
        qp = sb("qp", [P, NP, T], BF16)
        vst = sb("vst", [P, SC, P])
        vtile = sb("vtile", [P, SC, NH, QT])
        q_st = sb("q_st", [P, NH, T], BF16)
        k_st = sb("k_st", [P, NH, S], BF16)
        probs = sb("probs", [P, 2, GH, SC * T])
        o_sb = sb("o_sb", [P, NG, T])
        rs1 = sb("rs1", [P, TC, NH])
        on = sb("on", [P, TC, P])
        onT = sb("onT", [P, T])
        y_sb = sb("y_sb", [P, TC, P])
        mx = sb("mx", [P, TC, NH])
        mr = sb("mr", [P, 2, TC, GH])
        mparts = sb("mparts", [P, TC, NP, GH], BF16)
        mT = sb("mT", [NP * GH, 2, T], BF16)

        ps = ctx.enter_context(nc.psum_tensor("ps", [P, 8, 512], F32))
        SB, XB, OB, BB, FB = 0, 2, 4, (5, 7), 6

        q_scr = nc.dram_tensor("q_scr", (NP, DH, NH, T), BF16, kind="Internal").ap()
        k_scr = nc.dram_tensor("k_scr", (DH, NP, NH, S), BF16, kind="Internal").ap()

        s_rows = sem("s_rows")
        s_wall = sem("s_wall")
        s_ident = sem("s_ident")
        s_const = sem("s_const")
        s_early = sem("s_early")
        s_brows = sem("s_brows")
        s_gw2h = sem("s_gw2h")
        s_bcur = sem("s_bcur")
        s_xa = sem("s_xa")
        s_zero = sem("s_zero")
        s_ones = sem("s_ones")
        s_pp = sem("s_pp")
        s_pv = sem("s_pv")
        s_ps = sem("s_ps")
        s_x = sem("s_x")
        s_c = sem("s_c")
        s_var_a = sem("s_var_a")
        s_rstd_a = sem("s_rstd_a")
        s_var_b = sem("s_var_b")
        s_rstd_b = sem("s_rstd_b")
        s_xn = sem("s_xn")
        s_cn = sem("s_cn")
        s_full = [sem("s_full0"), sem("s_full1"), sem("s_full2")]
        s_done = [sem("s_done0"), sem("s_done1"), sem("s_done2")]
        s_nm0 = sem("s_nm0")
        s_p0 = sem("s_p0")
        s_tz = sem("s_tz")
        s_rd = sem("s_rd")
        s_re = sem("s_re")
        s_tg = sem("s_tg")
        s_x1 = sem("s_x1")
        s_xn1 = sem("s_xn1")
        s_res = sem("s_res")
        s_kp = sem("s_kp")
        s_qp = sem("s_qp")
        s_kscr = sem("s_kscr")
        s_qscr = sem("s_qscr")
        s_st = [sem("s_stA"), sem("s_stB")]
        s_vt = sem("s_vt")
        s_sc = sem("s_sc")
        s_pe = sem("s_pe")
        s_o = sem("s_o")
        s_od = sem("s_od")
        s_post = sem("s_post")
        s_pd = sem("s_pd")
        s_y = sem("s_y")
        s_out = sem("s_out")
        s_xf = [sem("s_xf0"), sem("s_xf1")]
        s_xd = [sem("s_xd0"), sem("s_xd1")]
        s_mp = sem("s_mp")
        s_mrow = [sem("s_mrow0"), sem("s_mrow1")]
        s_cv = sem("s_cv")
        s_cf = sem("s_cf")
        s_cur = sem("s_cur")
        s_ada = sem("s_ada")
        s_mqk = sem("s_mqk")
        s_cm = sem("s_cm")
        s_cx = sem("s_cx")
        s_cc = sem("s_cc")
        s_cg = sem("s_cg")
        s_tick = sem("s_tick")

        free_again = [*s_done, s_o, s_od, s_pe, s_y, s_x1, s_kscr, s_qscr,
                      *s_st, s_sc, *s_xd, *s_mrow, s_res, s_vt, s_out, s_pd]
        NWALL = 14
        ST_DMAS = 2

        def need(eng, s, value, hold=False):
            if isinstance(value, int) and value <= 0:
                return
            if s in free_again:
                value = value + CREDIT
            eng.wait_ge(s, value)
            if hold:
                eng.sem_inc(s_tick, 1)

        def full(eng, b, name, hold=False):
            q, per, k = turn_of(name)
            need(eng, s_full[q], b * per + k + 1, hold)

        def done(eng, b, name, hold=False):
            q, per, k = turn_of(name)
            need(eng, s_done[q], b * per + k + 1, hold)

        def room(eng, b, name):
            q, per, k = turn_of(name)
            need(eng, s_done[q], b * per + k)

        def bank(name):
            q, _, _ = turn_of(name)
            return ps[:, FB if q == 2 else BB[q], :]

        def filled(name, ins):
            ins.then_inc(s_full[turn_of(name)[0]], 1)

        def emptied(name, ins):
            ins.then_inc(s_done[turn_of(name)[0]], 1)

        def chunks(name):
            return bank(name).rearrange("p (c t) -> p c t", c=SC)

        def ada_col(k):
            return cur[:, k:k + 1]

        LEAVING = {
            "ctxT": (ctxT[:], bank("ctxT"), None, None),
            "nxT": (nxT[:], bank("nxT")[:, 0:T], early_cols[:, R_GAMMA:R_GAMMA + 1], early_cols[:, R_BETA:R_BETA + 1]),
            "qm": (qmT[:], bank("qm")[:, 0:T], None, None),
            "p0T_0": (p0T[:, :, 0:P], chunks("p0T_0"), None, None),
            "p0T_1": (p0T[:, :, P:T], chunks("p0T_1"), None, None),
            "pc": (pcT[:], bank("pc")[:, 0:T], None, None),
            "hkvT": (xkvT[:], bank("hkvT"), ada_col(2), ada_col(3)),
            "kproj": (kf[:], bank("kproj"), None, cols[:, R_BK:R_BK + 1]),
            "vproj": (vst[:].rearrange("p c d -> p (c d)"), bank("vproj"), None, None),
            "xqT": (xqT[:], bank("xqT")[:, 0:T], ada_col(0), ada_col(1)),
        }

        block = ctx.enter_context(nc.Block())

        @block.sync
        def _(sp):
            def v(name, r):
                return a[name].rearrange("(r d) -> r d", r=r)

            def at(t, b):
                return t[b:b + 1] if isinstance(b, int) else t[bass.ds(b, 1)]

            def waits(*pairs):
                for s, x in pairs:
                    need(sp, s, x, hold=not isinstance(x, int))

            def load(b, _):
                q, per, k = turn_of("pc")
                waits((s_done[q], (b - 1) * per + k + 1), (s_cn, b))
                sp.dma_start(x_sb[:], at(a["x"].rearrange("b (c p) d -> b p c d", p=P), b)).then_inc(s_x, 16)
                sp.dma_start(c_sb[:], at(a["ctx_1024"].rearrange("b (c p) d -> b p c d", p=P), b)).then_inc(s_c, 16)

            def load_x(b, _):
                waits((s_x1, b))
                if isinstance(b, int) and b == 0:
                    sp.wait_ge(s_pv, PV_ROWS)
                    for i in range(NP):
                        sp.dma_start(bias_cur[i:i + 1, :, :], bias_t[i * NCB:i * NCB + NBZ, :]).then_inc(s_bcur, 16)
                    sp.dma_start(bias_rows[:], bias_t[:]).then_inc(s_brows, 16)
                else:
                    columns = slice(b * NBZ, (b + 1) * NBZ) if isinstance(b, int) else bass.ds(b * NBZ, NBZ)
                    sp.wait_ge(s_brows, 16)
                    sp.dma_start(bias_cur[:], bias_rows[:, columns, :]).then_inc(s_bcur, 16)
                sp.dma_start(x_again[:], at(a["x"].rearrange("b (c p) d -> b p c d", p=P), b)).then_inc(s_xa, 16)

            def k_out(b, _):
                waits((s_kp, b + 1), *[(s_st[half], b * ST_DMAS * 16) for half in range(2)])
                for i in range(NP):
                    sp.dma_start(k_scr[:, i, :, :].rearrange("d h t -> h d t"), kp[:, i, :]).then_inc(s_kscr, 16)

            def q_out(b, _):
                waits((s_qp, b + 1), *[(s_st[half], b * ST_DMAS * 16) for half in range(2)])
                for i in range(NP):
                    sp.dma_start(q_scr[i].rearrange("d h t -> h d t"), qp[:, i, :]).then_inc(s_qscr, 16)

            def k_in(b, half):
                h0, h1 = half * NH // 2, (half + 1) * NH // 2
                waits((s_kscr, (b + 1) * NP * 16), (s_sc, (b - 1) * NU + 2 * h1))
                sp.dma_start(k_st[0:KR, h0:h1, :],
                             k_scr[:, :, h0:h1, :].rearrange("d j h t -> d j (h t)").unsqueeze(0)
                             .to_broadcast([NP, DH, NP, NH // 2 * S])).then_inc(s_st[half], 16)

            def q_in(b, half):
                h0, h1 = half * NH // 2, (half + 1) * NH // 2
                waits((s_qscr, (b + 1) * NP * 16), (s_sc, (b - 1) * NU + 2 * h1))
                sp.dma_start(q_st[0:KR, h0:h1, :],
                             q_scr[:, :, h0:h1, :].rearrange("i d h t -> i d (h t)").unsqueeze(2)
                             .to_broadcast([NP, DH, NP, NH // 2 * T])).then_inc(s_st[half], 16)

            def rows(b, g):
                m = MAXIMA.index(("rows", g))
                waits((s_xd[m % 2], b * MHALF + m // 2 + 1), (s_sc, (b - 1) * NU + 2 * GH * (g + 1)))
                sp.dma_start(q_st[KR:KR + NP, g * GH:(g + 1) * GH, :], mT[:, g % 2, :]).then_inc(s_mrow[g % 2], 16)

            def store(b, _):
                waits((s_y, b + 1))
                sp.dma_start(at(out.rearrange("b (c p) d -> b p c d", p=P), b), y_sb[:]).then_inc(s_out, 16)

            shares = dict(load=load, load_x=load_x, k_out=k_out, k_in=k_in,
                          q_out=q_out, q_in=q_in, rows=rows, store=store)

            load(0, 0)
            for k, name in ((R_GAMMA, "L0_xcond_ln_gamma"), (R_BETA, "L0_xcond_ln_beta")):
                sp.dma_start(early_rows[k:k + 1, :], v(name, 1)).then_inc(s_early, 16)
            for i, name in enumerate(("L0_xcond_Wq", "L0_xcond_Wk", "L0_xcond_Wv")):
                sp.dma_start(w_qkv[:, i, :], a[name]).then_inc(s_early, 16)
            for k in (1, 2, 0):
                sp.dma_start(w1[:, k, :, :], a["L0_xcond_e_w1"].rearrange("e (k c) r -> k c e r", k=3)[k])\
                    .then_inc(s_wall, 16)
            sp.dma_start(gw1[:], a["L0_xcond_gate_w1"].rearrange("(k c) r -> c k r", k=3)).then_inc(s_wall, 16)
            sp.dma_start(rw[:], a["L0_xcond_router_W"].rearrange("(k c) r -> c k r", k=3)).then_inc(s_wall, 16)
            sp.dma_start(w2[:], a["L0_xcond_e_w2"].rearrange("e (k r) h -> r (e k) h", k=RC)).then_inc(s_wall, 16)
            sp.dma_start(vec_rows[R_B1:R_B1 + E * RC, :],
                         a["L0_xcond_e_b1"].rearrange("e (k r) -> (e k) r", k=RC)).then_inc(s_rows, 16)
            for r, n, name in ((R_GB1, 1, "L0_xcond_gate_b1"), (R_BQ, 1, "L1_xcond_bq"), (R_BK, 2, "L1_xcond_bkv"),
                               (R_SSQ, 2, "L1_xcond_bss_q"), (R_SSK, 2, "L1_xcond_bss_kv"),
                               (R_OB, 1, "L0_xcond_out_b"), (R_GB2, 1, "L0_xcond_gate_b2"), (R_BP, 1, "L1_xcond_bp")):
                sp.dma_start(vec_rows[r:r + n, :], v(name, n)).then_inc(s_rows, 16)
            sp.dma_start(vec_rows[R_COND:R_COND + B, :], a["cond_1024"]).then_inc(s_rows, 16)
            sp.dma_start(vec_rows[R_EB2:R_EB2 + E, :], a["L0_xcond_e_b2"]).then_inc(s_rows, 16)
            for t, name in ((ow, "L0_xcond_out_w"), (wssq, "L1_xcond_Wss_q"), (wssk, "L1_xcond_Wss_kv"),
                            (wp1, "L1_xcond_Wp"), (gw2, "L0_xcond_gate_w2"), (wq1, "L1_xcond_Wq"),
                            (wkv1, "L1_xcond_Wkv")):
                sp.dma_start(t[:], a[name]).then_inc(s_wall, 16)
            sp.dma_start(rb[:], v("L0_xcond_router_b", E)).then_inc(s_wall, 16)
            sp.wait_ge(s_const, 1)
            sp.wait_ge(s_zero, 1)
            sp.dma_start(k_st[KR:KR + NP, :, :], onesb[:]).then_inc(s_ones, 16)
            load_x(0, 0)
            walk(shares, first_period("sp"), None, 0, 1)
            with sp.Fori(0, B - 2) as i:
                walk(shares, ORDER["sp"], i, i + 1, i + 2)
            walk(shares, last_but_one_period("sp"), B - 2, B - 1, None)
            walk(shares, last_period("sp"), B - 1, None, None)
            need(sp, s_out, 16 * B)

        @block.gpsimd
        def _(pool):
            own = Chain(pool, s_cg, 5)

            def stage(b, name):
                if name == "start":
                    need(pool, s_var_a, b + 1)
                    nc.gpsimd.tensor_tensor(rstd[:], ve[:], mhalf[:], ALU.pow).then_inc(s_rstd_a, 1)
                elif name == "xn":
                    full(pool, b - 1, "hkvT", hold=True)
                    need(pool, s_rstd_a, b + 1, hold=True)
                    for c in range(SC):
                        last = nc.gpsimd.tensor_scalar(cn[:, c, :], c_sb[:, c, :], mv[:, TC + c, 0:1],
                                                       rstd[:, TC + c:TC + c + 1], ALU.subtract, ALU.mult)
                    last.then_inc(s_cn, 1)
                elif name == "hkvT":
                    own.begin(b)
                elif name == "x1":
                    need(pool, s_var_b, b + 1)
                    own.step(nc.gpsimd.tensor_tensor(rstd1[:], ve1[:], mhalf[:, 0:TC], ALU.pow))
                    own.wait()
                    pool.sem_inc(s_rstd_b, 1)

            def k_part(b, n):
                if n == 0:
                    need(pool, s_kscr, b * NP * 16, hold=True)
                    done(pool, b, "kproj", hold=True)
                else:
                    own.wait()
                    pool.sem_inc(s_tick, 1)
                i = n // 2
                rest = kf[:] if i == 0 else kr[:, i - 1, :]
                if n == 2 * NP - 2:
                    nc.gpsimd.tensor_copy(kp[:, i, :], rest).then_inc(s_kp, 1)
                elif n % 2 == 1:
                    own.step(nc.gpsimd.tensor_tensor(kr[:, i, :], rest, kp[:, i, :], ALU.subtract))
                else:
                    own.step(nc.gpsimd.tensor_copy(kp[:, i, :], rest))

            def residual(b, _):
                need(pool, s_y, b, hold=True)
                nc.gpsimd.tensor_copy(resid[:], x1[:]).then_inc(s_res, 1)
                own.end()

            def values(b, _):
                done(pool, b, "vproj", hold=True)
                need(pool, s_o, NG * b, hold=True)
                nc.gpsimd.tensor_copy(vtile[:, :, :, 0:DH], vst[:].rearrange("p c (h d) -> p c h d", h=NH))\
                    .then_inc(s_vt, 1)

            def prep(_, n):
                if n == 4:
                    pool.wait_ge(s_cn, 1)
                    nc.gpsimd.memset(k_st[64:P, :, :].rearrange("p h t -> p (h t)").bitcast(F32), 0.0)
                    nc.gpsimd.memset(q_st[64:P, :, :].rearrange("p h t -> p (h t)").bitcast(F32), 0.0)\
                        .then_inc(s_zero, 1)
                elif n == 7:
                    pool.wait_ge(s_zero, 1)
                    pool.wait_ge(s_wall, 16 * NWALL)
                    nc.gpsimd.tensor_scalar(gw2h[:], gw2[:], 0.5, None, ALU.mult).then_inc(s_gw2h, 1)

            shares = dict(stage=stage, k_part=k_part, resid=residual, values=values, prep=prep)

            for s in free_again:
                pool.sem_inc(s, CREDIT)
            nc.gpsimd.memset(ident[:], 0.0).then_inc(s_cc, 1)
            pool.wait_ge(s_cc, 1)
            nc.gpsimd.affine_select(out=ident[:], in_=ident[:], compare_op=ALU.not_equal, fill=1.0, base=0,
                                    pattern=[[-1, P]], channel_multiplier=1).then_inc(s_ident, 1)
            nc.gpsimd.memset(biases[:], 0.0)
            nc.gpsimd.memset(onesb[:], 1.0)
            nc.gpsimd.memset(mhalf[:], -0.5)
            nc.gpsimd.memset(vtile[:], 0.0).then_inc(s_cc, 1)
            pool.wait_ge(s_cc, 2)
            pool.wait_ge(s_ident, 1)
            nc.gpsimd.tensor_copy(identb[:], ident[:])
            nc.gpsimd.memset(vtile[:, :, :, DH:DH + 1], 1.0).then_inc(s_const, 1)
            walk(shares, first_period("pool"), None, 0, 1)
            with pool.Fori(0, B - 2) as i:
                walk(shares, ORDER["pool"], i, i + 1, i + 2)
            walk(shares, last_but_one_period("pool"), B - 2, B - 1, None)
            walk(shares, last_period("pool"), B - 1, None, None)

        @block.scalar
        def _(act):
            def stage(b, name):
                for leaving in [name] if name in LEAVING else []:
                    if leaving in BY_SCALARE:
                        to, source, scale, bias = LEAVING[leaving]
                        if leaving in ("hkvT", "xqT"):
                            need(act, s_cur, b + 1)
                        if leaving in ("nxT", "pc"):
                            full(act, b - 1, "hid_3")
                        if leaving == "nxT":
                            act.wait_ge(s_pv, PV_EARLY)
                        full(act, b, leaving)
                        if name == "vproj":
                            need(act, s_vt, b, hold=True)
                        if scale is None and bias is None:
                            emptied(leaving, nc.scalar.copy(to, source))
                        else:
                            emptied(leaving, nc.scalar.activation(to, source, ACT.Identity, bias=bias,
                                                                  scale=1.0 if scale is None else scale))
                if name in ("s0_0", "s0_1"):
                    t = int(name[-1])
                    need(act, s_nm0, TC * b + t + 1)
                    emptied(name, nc.scalar.activation(p0[:, t, :], bank(name), ACT.Exp, bias=nm0[:, t:t + 1],
                                                       accum_out=sum0[:, t:t + 1]))
                elif name in HIDDEN:
                    k = HIDDEN.index(name)
                    n = min(2, NZ - 2 * k)
                    full(act, b, name)
                    nc.scalar.activation(tz[:, 2 * k:2 * k + n, :].rearrange("p z t -> p (z t)"),
                                         bank(name)[:, 0:n * T], ACT.Tanh, scale=0.5).then_inc(s_tz, 1)
                elif name == "route":
                    need(act, s_rd, b + 1)
                    nc.scalar.activation(re[:], rd[:], ACT.Exp).then_inc(s_re, 1)
                elif name in ("eo_0", "eo_1"):
                    full(act, b, name)
                    nc.scalar.activation(tg[:, int(name[-1]), :], bank(name)[:, E * P:], ACT.Tanh, scale=0.5)\
                        .then_inc(s_tg, 1)

            def unit(b, u):
                h, half = divmod(u, 2)
                g, j = divmod(h, GH)
                if u % (2 * GH) == 0:
                    need(act, s_o, NG * b + g - 1, hold=True)
                need(act, s_sc, NU * b + u + 1)
                nc.scalar.activation(probs[:, g % 2, j, half * 2 * T:(half + 1) * 2 * T], ps[:, SB + u % 2, :],
                                     ACT.Exp).then_inc(s_pe, 1)

            shares = dict(stage=stage, unit=unit)
            def prep(_, n):
                if n == 4:
                    act.wait_ge(s_pp, PREP.index(4) + 1)
                    nc.scalar.copy(cols[:], ps[:, 7, 0:NR]).then_inc(s_ps, 1)
                    act.wait_ge(s_ps, 1)
                    nc.scalar.activation(silu_t[:], cols[:, R_COND:R_COND + B], ACT.Tanh, scale=0.5)\
                        .then_inc(s_ps, 1)

            shares["prep"] = prep
            walk(shares, first_period("act"), None, 0, 1)
            with act.Fori(0, B - 2) as i:
                walk(shares, ORDER["act"], i, i + 1, i + 2)
            walk(shares, last_but_one_period("act"), B - 2, B - 1, None)
            walk(shares, last_period("act"), B - 1, None, None)

        @block.tensor
        def _(pe):
            def mm(out, lhsT, rhs, start=True, stop=True):
                return nc.tensor.matmul(out, lhsT, rhs, start=start, stop=stop)

            def turn(out, in_, idn):
                return nc.tensor.transpose(out, in_, idn)

            def prep(_, n):
                if n == 1:
                    pe.wait_ge(s_early, 16 * 5)
                    turn(ps[:, 0, 2 * P:2 * P + 2], early_rows[:], ident[0:2, 0:2])
                    for i in range(2):
                        last = turn(ps[:, 0, i * P:(i + 1) * P], w_qkv[:, i, :], ident[:])
                elif n == 2:
                    pe.wait_ge(s_pv, PV_EARLY)
                    last = mm(ps[:, 1, 0:P], w_qkvT[:, 0, :], w_qkvT[:, 1, :])
                elif n == 3:
                    last = turn(ps[:, 0, 3 * P:4 * P], w_qkv[:, 2, :], ident[:])
                elif n == 4:
                    pe.wait_ge(s_rows, 16 * 11)
                    last = turn(ps[:, 7, 0:NR], vec_rows[:], ident[0:NR, 0:NR])
                elif n == 5:
                    pe.wait_ge(s_wall, 16 * NWALL)
                    pe.wait_ge(s_pv, PV_WV)
                    wv_t = w_qkvT[:, 2, :]
                    w1f = w1[:, 1, :, :].rearrange("p e r -> p (e r)")
                    mm(ps[:, 2, :], wv_t, w1f[:, 0:512])
                    mm(ps[:, 3, 0:256], wv_t, w1f[:, 512:768])
                    mm(ps[:, 3, 256:256 + P], wv_t, gw1[:, 1, :])
                    mm(ps[:, 3, 384:384 + E], wv_t, rw[:, 1, :])
                    for k in range(4):
                        turn(ps[:, 4, k * P:(k + 1) * P], w2[:, k, :], ident[:])
                    for k in range(2):
                        last = turn(ps[:, 5, k * P:(k + 1) * P], w2[:, 4 + k, :], ident[:])
                elif n == 6:
                    pe.wait_ge(s_ps, 1)
                    cond = cols[:, R_COND:R_COND + B]
                    for z in range(NZ):
                        lhsT = gw1[:, 2, :] if z == NZ - 1 else w1[:, 2, z // RC, z % RC * P:(z % RC + 1) * P]
                        mm(ps[:, 7, z * B:(z + 1) * B], lhsT, cond)
                    mm(ps[0:E, 7, NZ * B:NBZ * B], rw[:, 2, :], cond)
                    mm(ps[:, 7, C_EB:C_EB + E], ow[:], cols[:, R_EB2:R_EB2 + E])
                    mm(ps[:, 7, C_BO:C_BO + 1], wp1[:], cols[:, R_BV:R_BV + 1])
                    pe.wait_ge(s_pv, PV_SILU)
                    for k, w in enumerate((wssq, wssk)):
                        for j in range(2):
                            z = 2 * k + j
                            last = mm(ps[:, 7, 64 + z * B:64 + (z + 1) * B], w[:, j * P:(j + 1) * P], silu_c[:])
                elif n == 8:
                    for k in range(E * RC):
                        last = mm(ps[:, 2 + k // 4, k % 4 * P:(k % 4 + 1) * P], w2T[:, k, :], ow[:])
                elif n == 7:
                    pe.wait_ge(s_pv, PV_PARTS)
                    last = turn(ps[0:NP * NCB, 4, :].bitcast(BF16)[:, 0:P],
                                bias_p[:].rearrange("p i c -> p (i c)"), identb[:])
                last.then_inc(s_pp, 1)

            def bias(out, lhsT, rhs):
                mm(out, lhsT, rhs, stop=False)

            def stage(b, stage_name):
                def begin(name):
                    room(pe, b, name)
                    return bank(name)

                if stage_name == "ctxT":
                    o = begin("ctxT")
                    need(pe, s_c, 16 * (b + 1))
                    for c in range(SC):
                        last = turn(o[:, c * P:(c + 1) * P], c_sb[:, c, :], ident[:])
                    filled("ctxT", last)
                elif stage_name == "nxT":
                    o = begin("nxT")
                    need(pe, s_xn, b + 1)
                    for t in range(TC):
                        last = turn(o[:, t * P:(t + 1) * P], xn[:, t, :], ident[:])
                    filled("nxT", last)
                elif stage_name == "qm":
                    o = begin("qm")
                    if isinstance(b, int) and b == 0:
                        pe.wait_ge(s_mqk, 1)
                    done(pe, b, "nxT")
                    filled("qm", mm(o[:, 0:T], m_qk[:], nxT[:]))
                elif stage_name in ("s0_0", "s0_1"):
                    t = int(stage_name[-1])
                    o = begin(stage_name)
                    filled(stage_name, mm(o, qmT[:, t * P:(t + 1) * P], ctxT[:]))
                elif stage_name == "hkvT":
                    o = begin("hkvT")
                    if isinstance(b, int) and b == 0:
                        pe.wait_ge(s_pv, PV_ROWS)
                    need(pe, s_cn, b + 1)
                    for c in range(SC):
                        last = turn(o[:, c * P:(c + 1) * P], cn[:, c, :], ident[:])
                    filled("hkvT", last)
                elif stage_name == "kproj":
                    o = begin("kproj")
                    done(pe, b, "hkvT")
                    filled("kproj", mm(o, wkv1[:, 0:P], xkvT[:]))
                elif stage_name in ("p0T_0", "p0T_1"):
                    t = int(stage_name[-1])
                    o = begin(stage_name)
                    need(pe, s_p0, TC * b + t + 1)
                    for c in range(SC):
                        last = turn(o[:, c * P:(c + 1) * P], p0[:, t, c * P:(c + 1) * P], ident[:])
                    filled(stage_name, last)
                elif stage_name == "vproj":
                    o = begin("vproj")
                    for c in range(SC):
                        last = mm(o[:, c * P:(c + 1) * P], xkvT[:, c * P:(c + 1) * P], wkv1[:, P:2 * P])
                    filled("vproj", last)
                elif stage_name == "pc":
                    o = begin("pc")
                    done(pe, b, "p0T_1")
                    for c in range(SC):
                        last = mm(o[:, 0:T], c_sb[:, c, :], p0T[:, c, :], start=(c == 0), stop=(c == SC - 1))
                    filled("pc", last)
                elif stage_name == "lgT":
                    o = begin("lgT")
                    need(pe, s_bcur, 16 * (b + NP))
                    done(pe, b, "pc")
                    for t in range(TC):
                        ot = o[:, t * E:(t + 1) * E]
                        bias(ot, onesb[0:NP, 0:P], bias_cur[:, NZ, 0:E])
                        mm(ot, nxT[:, t * P:(t + 1) * P], rw[:, 0, :], start=False, stop=False)
                        last = mm(ot, pcT[:, t * P:(t + 1) * P], rwev[:], start=False)
                    filled("lgT", last)
                elif stage_name in HIDDEN:
                    k = HIDDEN.index(stage_name)
                    o = begin(stage_name)
                    for z in range(2 * k, min(2 * k + 2, NZ)):
                        if z < NZ - 1:
                            wa, wb = w1[:, 0, z // RC, z % RC * P:(z % RC + 1) * P], w1ev[:, z * P:(z + 1) * P]
                        else:
                            wa, wb = gw1[:, 0, :], gw1ev[:]
                        oz = o[:, (z - 2 * k) * T:(z - 2 * k + 1) * T]
                        bias(oz, bias_cur[:, z, :], onesb[0:NP, :])
                        mm(oz, wa, nxT[:], start=False, stop=False)
                        last = mm(oz, wb, pcT[:], start=False)
                    filled(stage_name, last)
                elif stage_name in ("eo_0", "eo_1"):
                    t = int(stage_name[-1])
                    if isinstance(b, int) and b == 0:
                        pe.wait_ge(s_gw2h, 1)
                        pe.wait_ge(s_pv, PV_ALL)
                    o = begin(stage_name)
                    done(pe, b, "hid_3" if t == 0 else "hid_2")
                    pe.wait_ge(s_brows, 16)
                    bias(o, onesb[0:NP, 0:P], bias_rows[:, C_EB:C_EB + E + 1, :].rearrange("p c n -> p (c n)"))
                    for e in range(E):
                        for k in range(RC):
                            mm(o[:, e * P:(e + 1) * P], hT[:, e * RC + k, t * P:(t + 1) * P],
                               w2o[:, e * RC + k, :], start=False, stop=False)
                    filled(stage_name, mm(o[:, E * P:], hT[:, NZ - 1, t * P:(t + 1) * P], gw2h[:], start=False))
                elif stage_name == "xqT":
                    o = begin("xqT")
                    need(pe, s_xn1, b + 1)
                    for t in range(TC):
                        last = turn(o[:, t * P:(t + 1) * P], xn1[:, t, :], ident[:])
                    filled("xqT", last)
                elif stage_name == "qproj":
                    o = begin("qproj")
                    done(pe, b, "xqT")
                    filled("qproj", mm(o[:, 0:T], wq1[:], xqT[:]))

            def maxima_bank(b, m):
                need(pe, s_xd[m % 2], b * MHALF + m // 2, hold=True)
                return ps[:, XB + m % 2, :]

            def tile(b, gk):
                g, k = gk
                h, t = g * GH + k // TC, k % TC
                m = MAXIMA.index(("tile", gk))
                if k == 0:
                    need(pe, s_st[g // 2], (b + 1) * ST_DMAS * 16, hold=True)
                o = maxima_bank(b, m)
                mm(o, q_st[0:KR, h, t * P:(t + 1) * P], k_st[0:KR, h, :]).then_inc(s_xf[m % 2], 1)

            def rows(b, g):
                m = MAXIMA.index(("rows", g))
                need(pe, s_mp, NG * b + g + 1, hold=True)
                o = maxima_bank(b, m)[0:NP * GH, :].bitcast(BF16)
                for t in range(TC):
                    last = turn(o[:, t * P:(t + 1) * P],
                                mparts[:, t, :, :].rearrange("p i h -> p (i h)"), identb[:])
                last.then_inc(s_xf[m % 2], 1)

            def unit(b, u):
                h, half = divmod(u, 2)
                g = h // GH
                if u == 0:
                    pe.wait_ge(s_ones, 16)
                if u % (2 * GH) == 0:
                    need(pe, s_mrow[g % 2], 16 * (2 * b + g // 2 + 1), hold=True)
                need(pe, s_pe, NU * b + u - 1)
                for j in range(2):
                    c = 2 * half + j
                    last = mm(ps[:, SB + u % 2, j * T:(j + 1) * T], k_st[:, h, c * P:(c + 1) * P], q_st[:, h, :])
                last.then_inc(s_sc, 1)

            def pv(b, g):
                if g == 0:
                    need(pe, s_vt, b + 1)
                need(pe, s_pe, NU * b + 2 * (g + 1) * GH)
                need(pe, s_od, NG * b + g)
                need(pe, s_pd, 4 * b)
                for c in range(SC):
                    for j in range(GH):
                        last = mm(ps[j * QT:(j + 1) * QT, OB, 0:T], vtile[:, c, g * GH + j, :],
                                  probs[:, g % 2, j, c * T:(c + 1) * T], start=(c == 0), stop=(c == SC - 1))
                last.then_inc(s_o, 1)

            def after(b, n):
                need(pe, s_pd, 4 * b + n)
                if n < 2:
                    t = n
                    need(pe, s_od, NG * (b + 1))
                    for g in range(NG):
                        last = turn(ps[:, OB, g * P:(g + 1) * P], o_sb[:, g, t * P:(t + 1) * P], ident[:])
                elif n == 2:
                    for t in range(TC):
                        last = turn(ps[:, OB, t * P:(t + 1) * P], on[:, t, :], ident[:])
                else:
                    for t in range(TC):
                        bias(ps[:, OB, t * P:(t + 1) * P], onesb[0:NP, 0:P], bias_rows[:, C_BO, :])
                        last = mm(ps[:, OB, t * P:(t + 1) * P], onT[:, t * P:(t + 1) * P], wp1[:], start=False)
                last.then_inc(s_post, 1)

            shares = dict(stage=stage, prep=prep, tile=tile, rows=rows, unit=unit, pv=pv, after=after)
            pe.wait_ge(s_ident, 1)
            walk(shares, first_period("pe"), None, 0, 1)
            with pe.Fori(0, B - 2) as i:
                walk(shares, ORDER["pe"], i, i + 1, i + 2)
            walk(shares, last_but_one_period("pe"), B - 2, B - 1, None)
            walk(shares, last_period("pe"), B - 1, None, None)

        @block.vector
        def _(dve):
            V = nc.vector

            steps = Chain(dve, s_pv, PV_ALL)
            steps.begin(0)

            def prep(_, n):
                dve.wait_ge(s_pp, PREP.index(n) + 1)
                if n == 1:
                    V.tensor_copy(early_cols[:], ps[:, 0, 2 * P:2 * P + 2])
                    steps.step(V.tensor_copy(w_qkvT[:, 0:2, :].rearrange("p a n -> p (a n)"), ps[:, 0, 0:2 * P]))
                    assert steps.n == PV_EARLY
                elif n == 2:
                    V.tensor_scalar(m_qk[:], ps[:, 1, 0:P], SCALE0, None, ALU.mult).then_inc(s_mqk, 1)
                elif n == 3:
                    steps.step(V.tensor_copy(w_qkvT[:, 2, :], ps[:, 0, 3 * P:4 * P]))
                    assert steps.n == PV_WV
                elif n == 4:
                    dve.wait_ge(s_ps, 2)
                    steps.step(V.scalar_tensor_tensor(silu_c[:], silu_t[:], 1.0, cols[:, R_COND:R_COND + B],
                                                      ALU.add, ALU.mult))
                    assert steps.n == PV_SILU
                elif n == 5:
                    V.tensor_copy(w1ev[:, 0:512], ps[:, 2, :])
                    V.tensor_copy(w1ev[:, 512:768], ps[:, 3, 0:256])
                    V.tensor_copy(gw1ev[:], ps[:, 3, 256:384])
                    V.tensor_copy(rwev[:], ps[:, 3, 384:384 + E])
                    V.tensor_copy(w2T[:, 0:4, :].rearrange("p a n -> p (a n)"), ps[:, 4, :])
                    steps.step(V.tensor_copy(w2T[:, 4:6, :].rearrange("p a n -> p (a n)"), ps[:, 5, 0:256]))
                    assert steps.n == PV_W2T
                elif n == 6:
                    dve.wait_ge(s_const, 1)
                    by_batch = biases[:, 0:C_EB].rearrange("p (b z) -> p z b", z=NBZ)
                    V.tensor_tensor(by_batch[:, 0:NZ, :], ps[:, 7, 0:NZ * B].rearrange("p (z b) -> p z b", b=B),
                                    cols[:, R_B1:R_B1 + NZ].unsqueeze(2).to_broadcast([P, NZ, B]), ALU.add)
                    V.tensor_scalar(by_batch[0:E, NZ, :], ps[0:E, 7, NZ * B:NBZ * B], rb[:, 0:1], None, ALU.add)
                    V.tensor_scalar(biases[:, C_EB:C_EB + E], ps[:, 7, C_EB:C_EB + E], cols[:, R_OB:R_OB + 1], None,
                                    ALU.add)
                    V.tensor_copy(biases[:, C_GB:C_GB + 1], cols[:, R_GB2:R_GB2 + 1])
                    steps.link(V.tensor_scalar(biases[:, C_BO:C_BO + 1], ps[:, 7, C_BO:C_BO + 1],
                                               cols[:, R_BP:R_BP + 1], None, ALU.add))
                    steps.link(V.tensor_copy(bias_p[:, 0, :], biases[:]))
                    steps.link(V.tensor_tensor(bias_r[:, 0, :], biases[:], bias_p[:, 0, :], ALU.subtract))
                    steps.link(V.tensor_copy(bias_p[:, 1, :], bias_r[:, 0, :]))
                    steps.link(V.tensor_tensor(bias_r[:, 1, :], bias_r[:, 0, :], bias_p[:, 1, :], ALU.subtract))
                    steps.step(V.tensor_copy(bias_p[:, 2, :], bias_r[:, 1, :]))
                    assert steps.n == PV_PARTS
                    ada_z = ada[:].rearrange("p b z -> p z b")
                    V.scalar_tensor_tensor(ada_z, ps[:, 7, 64:64 + NADA * B].rearrange("p (z b) -> p z b", b=B), 0.5,
                                           cols[:, R_SSQ:R_SSQ + NADA].unsqueeze(2).to_broadcast([P, NADA, B]),
                                           ALU.mult, ALU.add).then_inc(s_ada, 1)
                    dve.wait_ge(s_ada, 1)
                    for k in range(2):
                        V.tensor_scalar(ada[:, :, 2 * k:2 * k + 1], ada[:, :, 2 * k:2 * k + 1], 1.0, None, ALU.add)\
                            .then_inc(s_ada, 1)
                elif n == 7:
                    steps.step(V.tensor_copy(bias_t[:], ps[0:NP * NCB, 4, :].bitcast(BF16)[:, 0:P]))
                    assert steps.n == PV_ROWS
                else:
                    V.tensor_scalar(w2o[:, 0:4, :].rearrange("p a n -> p (a n)"), ps[:, 2, :], 0.5, None, ALU.mult)
                    steps.link(V.tensor_scalar(w2o[:, 4:6, :].rearrange("p a n -> p (a n)"), ps[:, 3, 0:256], 0.5,
                                               None, ALU.mult))
                    steps.end()

            own = Chain(dve, s_cv, 16)
            ahead = Chain(dve, s_cf, 4)
            late = Chain(dve, s_cm, 2)
            top = Chain(dve, s_cx, 4)

            def stage(b, stage_name):
                if stage_name == "hkvT":
                    own.begin(b)
                    at_b = slice(b, b + 1) if isinstance(b, int) else bass.ds(b, 1)
                    dve.wait_ge(s_ada, 3)
                    done(dve, b - 1, "xqT")
                    V.tensor_copy(cur[:], ada[:, at_b, :].rearrange("p a v -> p (a v)")).then_inc(s_cur, 1)
                for leaving in [stage_name] if stage_name in LEAVING else []:
                    if leaving not in BY_SCALARE:
                        to, source, scale, bias = LEAVING[leaving]
                        if leaving in ("hkvT", "xqT"):
                            need(dve, s_cur, b + 1)
                        if leaving in ("nxT", "pc"):
                            full(dve, b - 1, "hid_3")
                        full(dve, b, leaving)
                        if leaving == "kproj":
                            need(dve, s_kp, b)
                        if scale is not None:
                            ins = V.tensor_scalar(to, source, scale, bias, ALU.mult, ALU.add)
                        elif bias is not None:
                            ins = V.tensor_scalar(to, source, bias, None, ALU.add)
                        else:
                            ins = V.tensor_copy(to, source)
                        emptied(leaving, ins)
                if stage_name == "start":
                    ahead.begin(b)
                    need(dve, s_x, 16 * (b + 1))
                    need(dve, s_cn, b)
                    for t in range(TC):
                        V.bn_stats(stats[:, t, :], x_sb[:, t, :])
                    need(dve, s_c, 16 * (b + 1))
                    for c in range(SC):
                        last = V.bn_stats(stats[:, TC + c, :], c_sb[:, c, :])
                    ahead.step(last)
                    ahead.wait()
                    dve.sem_inc(s_tick, 1)
                    for t in range(TC + SC):
                        last = V.bn_aggr(mv[:, t, :], stats[:, t, :])
                    ahead.link(last)
                    V.tensor_scalar(ve[:], mv[:, :, 1], EPS, None, ALU.add).then_inc(s_var_a, 1)
                elif stage_name == "xn":
                    need(dve, s_rstd_a, b + 1)
                    for t in range(TC):
                        last = V.tensor_scalar(xn[:, t, :], x_sb[:, t, :], mv[:, t, 0:1], rstd[:, t:t + 1],
                                               ALU.subtract, ALU.mult)
                    last.then_inc(s_xn, 1)
                elif stage_name in ("s0_0", "s0_1"):
                    t = int(stage_name[-1])
                    full(dve, b, stage_name)
                    V.tensor_reduce(nm0[:, t:t + 1], bank(stage_name), AX_X, ALU.max, negate=True)\
                        .then_inc(s_nm0, 1)
                elif stage_name in ("p0_0", "p0_1"):
                    t = int(stage_name[-1])
                    done(dve, b, f"s0_{t}")
                    ahead.link(V.reciprocal(rs0[:, t:t + 1], sum0[:, t:t + 1]))
                    V.tensor_scalar(p0[:, t, :], p0[:, t, :], rs0[:, t:t + 1], None, ALU.mult).then_inc(s_p0, 1)
                elif stage_name == "pc":
                    ahead.end()
                elif stage_name in ACTIVATED:
                    k = ACTIVATED.index(stage_name)
                    name = HIDDEN[k]
                    n = min(2, NZ - 2 * k)
                    need(dve, s_tz, 4 * b + k + 1)
                    emptied(name, V.scalar_tensor_tensor(
                        hT[:, 2 * k:2 * k + n, :].rearrange("p z t -> p (z t)"),
                        tz[:, 2 * k:2 * k + n, :].rearrange("p z t -> p (z t)"), 1.0, bank(name)[:, 0:n * T],
                        ALU.add, ALU.mult))
                elif stage_name == "lgT":
                    full(dve, b, "lgT")
                    lgT = bank("lgT")[:, 0:TC * E].rearrange("p (t e) -> p t e", e=E)
                    own.link(V.tensor_reduce(rmx[:], lgT, AX_X, ALU.max))
                    emptied("lgT", V.tensor_tensor(rd[:], lgT, rmx[:].unsqueeze(2).to_broadcast([P, TC, E]),
                                                   ALU.subtract))
                    done(dve, b, "lgT")
                    dve.sem_inc(s_rd, 1)
                elif stage_name == "route":
                    need(dve, s_re, b + 1)
                    own.link(V.tensor_reduce(rsum[:], re[:], AX_X, ALU.add))
                    own.link(V.reciprocal(rinv[:], rsum[:]))
                    own.link(V.tensor_tensor(pr[:], re[:], rinv[:].unsqueeze(2).to_broadcast([P, TC, E]), ALU.mult))
                elif stage_name in ("eo_0", "eo_1"):
                    t = int(stage_name[-1])
                    o = bank(stage_name)
                    need(dve, s_tg, TC * b + t + 1)
                    own.link(V.tensor_scalar(yacc[:, 0, t, :], o[:, 0:P], pr[:, t, 0:1], None, ALU.mult))
                    own.link(V.scalar_tensor_tensor(yacc[:, 1, t, :], o[:, P:2 * P], pr[:, t, 1:2],
                                                    yacc[:, 0, t, :], ALU.mult, ALU.add))
                    emptied(stage_name, V.scalar_tensor_tensor(yacc[:, 2, t, :], o[:, 2 * P:3 * P], pr[:, t, 2:3],
                                                               yacc[:, 1, t, :], ALU.mult, ALU.add))
                elif stage_name == "x1":
                    for t in range(TC):
                        done(dve, b, f"eo_{t}")
                    dve.sem_inc(s_tick, 1)
                    own.link(V.scalar_tensor_tensor(ug[:], tg[:], 1.0, yacc[:, E - 1, :, :], ALU.add, ALU.mult))
                    need(dve, s_res, b)
                    need(dve, s_xa, 16 * (b + 1))
                    own.step(V.scalar_tensor_tensor(x1[:], ug[:], 0.5, x_again[:], ALU.mult, ALU.add))
                    own.wait()
                    dve.sem_inc(s_x1, 1)
                    for t in range(TC):
                        last = V.bn_stats(st1[:, t, :], x1[:, t, :])
                    own.step(last)
                    own.wait()
                    dve.sem_inc(s_tick, 1)
                    for t in range(TC):
                        last = V.bn_aggr(mv1[:, t, :], st1[:, t, :])
                    own.link(last)
                    V.tensor_scalar(ve1[:], mv1[:, :, 1], EPS, None, ALU.add).then_inc(s_var_b, 1)
                elif stage_name == "xn1":
                    need(dve, s_rstd_b, b + 1)
                    for t in range(TC):
                        last = V.tensor_scalar(xn1[:, t, :], x1[:, t, :], mv1[:, t, 0:1], rstd1[:, t:t + 1],
                                               ALU.subtract, ALU.mult)
                    last.then_inc(s_xn1, 1)
                elif stage_name == "qproj":
                    full(dve, b, "qproj")
                    emptied("qproj", V.tensor_scalar(qf[:], bank("qproj")[:, 0:T], cols[:, R_BQ:R_BQ + 1], SCALE1,
                                                     ALU.add, ALU.mult))
                elif stage_name == "q_parts":
                    done(dve, b, "qproj")
                    need(dve, s_qscr, b * NP * 16)
                    own.link(V.tensor_copy(qp[:, 0, :], qf[:]))
                    own.link(V.tensor_tensor(qr[:, 0, :], qf[:], qp[:, 0, :], ALU.subtract))
                    own.link(V.tensor_copy(qp[:, 1, :], qr[:, 0, :]))
                    own.link(V.tensor_tensor(qr[:, 1, :], qr[:, 0, :], qp[:, 1, :], ALU.subtract))
                    V.tensor_copy(qp[:, 2, :], qr[:, 1, :]).then_inc(s_qp, 1)
                    own.end()

            def tile(b, gk):
                g, k = gk
                h, t = g * GH + k // TC, k % TC
                m = MAXIMA.index(("tile", gk))
                need(dve, s_xf[m % 2], b * MHALF + m // 2 + 1)
                V.tensor_reduce(mx[:, t, h:h + 1], ps[:, XB + m % 2, :], AX_X, ALU.max, negate=True)\
                    .then_inc(s_xd[m % 2], 1)

            def part(b, gn):
                g, n = gn
                mg = mx[:, :, g * GH:(g + 1) * GH]
                if n == 0:
                    top.begin(NG * b + g)
                    m = MAXIMA.index(("tile", (g, GH * TC - 1)))
                    for of_tile in (m, m - 1):
                        need(dve, s_xd[of_tile % 2], b * MHALF + of_tile // 2 + 1)
                    top.step(V.tensor_copy(mparts[:, :, 0, :], mg))
                else:
                    top.wait()
                    i = n // 2
                    rest = mg if i == 0 else mr[:, i - 1]
                    if n == 2 * NP - 2:
                        V.tensor_copy(mparts[:, :, i, :], rest).then_inc(s_mp, 1)
                        top.end()
                    elif n % 2 == 1:
                        top.step(V.tensor_tensor(mr[:, i], rest, mparts[:, :, i, :], ALU.subtract))
                    else:
                        top.step(V.tensor_copy(mparts[:, :, i, :], rest))

            def rows(b, g):
                m = MAXIMA.index(("rows", g))
                need(dve, s_mrow[g % 2], 16 * (2 * b + g // 2))
                need(dve, s_xf[m % 2], b * MHALF + m // 2 + 1)
                V.tensor_copy(mT[:, g % 2, :], ps[0:NP * GH, XB + m % 2, :].bitcast(BF16)[:, 0:T])\
                    .then_inc(s_xd[m % 2], 1)

            def pv(b, g):
                need(dve, s_o, NG * b + g + 1)
                V.tensor_copy(o_sb[:, g, :], ps[:, OB, 0:T]).then_inc(s_od, 1)

            def after(b, n):
                if n < 2:
                    t = n
                    if t == 0:
                        late.begin(b)
                    o = ps[:, OB, :].rearrange("p (h q) -> p h q", q=QT)
                    need(dve, s_post, 4 * b + t + 1)
                    late.link(V.reciprocal(rs1[:, t, :], o[:, :, DH]))
                    V.tensor_tensor(on[:, t, :].rearrange("p (h d) -> p h d", d=DH), o[:, :, 0:DH],
                                    rs1[:, t, :].unsqueeze(2).to_broadcast([P, NH, DH]), ALU.mult)\
                        .then_inc(s_pd, 1)
                elif n == 2:
                    need(dve, s_post, 4 * b + 3)
                    V.tensor_copy(onT[:], ps[:, OB, 0:T]).then_inc(s_pd, 1)
                else:
                    need(dve, s_post, 4 * b + 4)
                    need(dve, s_res, b + 1)
                    need(dve, s_out, 16 * b)
                    V.tensor_tensor(y_sb[:], ps[:, OB, 0:T].rearrange("p (t d) -> p t d", d=P), resid[:],
                                    ALU.add).then_inc(s_pd, 1)
                    need(dve, s_pd, 4 * b + 4)
                    dve.sem_inc(s_y, 1)
                    late.end()

            shares = dict(stage=stage, prep=prep, tile=tile, part=part, rows=rows, pv=pv, after=after)
            walk(shares, first_period("dve"), None, 0, 1)
            with dve.Fori(0, B - 2) as i:
                walk(shares, ORDER["dve"], i, i + 1, i + 2)
            walk(shares, last_but_one_period("dve"), B - 2, B - 1, None)
            walk(shares, last_period("dve"), B - 1, None, None)


_INS = [
    "x", "cond_1024", "ctx_1024", "L0_xcond_ln_gamma", "L0_xcond_ln_beta", "L0_xcond_Wq", "L0_xcond_Wk",
    "L0_xcond_Wv", "L0_xcond_router_W", "L0_xcond_router_b", "L0_xcond_e_w1", "L0_xcond_e_b1", "L0_xcond_e_w2",
    "L0_xcond_e_b2", "L0_xcond_gate_w1", "L0_xcond_gate_b1", "L0_xcond_gate_w2", "L0_xcond_gate_b2",
    "L0_xcond_out_w", "L0_xcond_out_b", "L1_xcond_Wq", "L1_xcond_bq", "L1_xcond_Wkv", "L1_xcond_bkv",
    "L1_xcond_Wp", "L1_xcond_bp", "L1_xcond_Wss_q", "L1_xcond_bss_q", "L1_xcond_Wss_kv", "L1_xcond_bss_kv",
]


def kernel(**inputs):
    import numpy as _np
    import concourse.bacc as _bacc
    from concourse import mybir as _mybir
    from concourse.bass_utils import run_bass_kernel_spmd as _run

    nc = _bacc.Bacc("TRN2", target_bir_lowering=False, num_devices=1)
    arrays, aps = {}, {}
    for name in _INS:
        array = _np.ascontiguousarray(inputs[name])
        arrays[f"in_{name}"] = array
        aps[name] = nc.dram_tensor(f"in_{name}", array.shape, _mybir.dt.from_np(array.dtype),
                                   kind="ExternalInput").ap()
    out = nc.dram_tensor("out_0", (B, T, P), _mybir.dt.float32, kind="ExternalOutput").ap()
    build(nc, aps, out)
    r = _run(nc, [arrays], core_ids=[0])
    return r.results[0]["out_0"]
```
